# Optimizing a Trainium2 kernel written in Bass

```python
import numpy as np
import jax
import jax.numpy as jnp

def _softmax(x, axis=-1):
    return jax.nn.softmax(x, axis=axis)

def _gelu(x):
    return jax.nn.gelu(x, approximate=True)

def _silu(x):
    return jax.nn.silu(x)

def _sigmoid(x):
    return jax.nn.sigmoid(x)

def _layernorm(x, axis=-1, eps=1e-05):
    m = jnp.mean(x, axis=axis, keepdims=True)
    v = jnp.var(x, axis=axis, keepdims=True)
    return (x - m) / jnp.sqrt(v + eps)

def _scatter_add(tgt, idx, src, axis=0):
    return tgt.at[idx].add(src)

def _segment_sum(src, seg, n):
    return jax.ops.segment_sum(src, seg, n)
kernel_name = 'mk_vit_tower_d4_tok_img768_r4_1d8bc5'

def setup_inputs(seed: int=0):
    np.random.seed(seed)
    _w = jnp.asarray

    def _rec_inputs():
        import jax
        import jax.numpy as jnp
        _rk = jax.random.key(seed)
        x = 7.57192e-06 + 1.00007 * jax.random.normal(jax.random.fold_in(_rk, 1), (32, 128, 128, 3), jnp.float32)
        return x
    x = _rec_inputs()

    def _L0_tok_setup():
        import jax, jax.numpy as jnp
        import numpy as np
        PATCH = 16
        EPS = 1e-05

        def _shifts(x):
            b, h, w, c = x.shape
            zc = jnp.zeros((b, h, 1, c), x.dtype)
            zr = jnp.zeros((b, 1, w, c), x.dtype)
            s_right = jnp.concatenate([zc, x[:, :, :-1, :]], axis=2)
            s_left = jnp.concatenate([x[:, :, 1:, :], zc], axis=2)
            s_down = jnp.concatenate([zr, x[:, :-1, :, :]], axis=1)
            s_up = jnp.concatenate([x[:, 1:, :, :], zr], axis=1)
            return [s_right, s_left, s_down, s_up]
        key = jax.random.key(seed)
        k1, k2 = jax.random.split(key)
        b, h, w, c, dim = (64, 224, 224, 3, 192)
        feat = PATCH * PATCH * 5 * c
        x = jax.random.normal(k1, (b, h, w, c), dtype=jnp.float32)
        ln_scale = jnp.ones((feat,), jnp.float32)
        W = jax.random.normal(k2, (feat, dim), dtype=jnp.float32) * (1.0 / np.sqrt(feat))
        bb = jnp.zeros((dim,), jnp.float32)
        return {'x': x, 'ln_scale': ln_scale, 'W': W, 'b': bb}
    _L0_tok_all = _L0_tok_setup()
    _L0_tok_in = {k: v for k, v in _L0_tok_all.items() if k in ('ln_scale', 'W', 'b')}
    del _L0_tok_all

    def _L0_attn_setup():
        import jax, jax.numpy as jnp
        import numpy as np
        import math
        DIM = 192
        NUM_HEADS = 12

        def _xavier_uniform(key, out_f, in_f):
            a = math.sqrt(6.0 / (in_f + out_f))
            return jax.random.uniform(key, (out_f, in_f), jnp.float32, -a, a)
        key = jax.random.key(seed)
        k_x, k_qw, k_qB, k_pw, k_pB = jax.random.split(key, 5)
        B, N = (16, 256)
        x = jax.random.normal(k_x, (B, N, DIM), jnp.float32)
        qkv_w = _xavier_uniform(k_qw, 3 * DIM, DIM)
        qkv_b = jnp.zeros((3 * DIM,), jnp.float32)
        qkv_B = jax.random.normal(k_qB, (3 * DIM, DIM), jnp.float32) * math.sqrt(1.0 / DIM)
        proj_w = _xavier_uniform(k_pw, DIM, DIM)
        proj_b = jnp.zeros((DIM,), jnp.float32)
        proj_B = jax.random.normal(k_pB, (DIM, DIM), jnp.float32) * math.sqrt(1.0 / DIM)
        return {'x': x, 'qkv_w': qkv_w, 'qkv_b': qkv_b, 'qkv_B': qkv_B, 'proj_w': proj_w, 'proj_b': proj_b, 'proj_B': proj_B}
    _L0_attn_all = _L0_attn_setup()
    _L0_attn_in = {k: v for k, v in _L0_attn_all.items() if k in ('qkv_w', 'qkv_b', 'qkv_B', 'proj_w', 'proj_b', 'proj_B')}
    del _L0_attn_all

    def _L0_ffn_setup():
        import jax, jax.numpy as jnp
        import numpy as np
        B, S, H, F, E, TOP_K = (4, 512, 192, 768, 8, 2)
        key = jax.random.key(seed)
        ks = jax.random.split(key, 6)
        x = jax.random.normal(ks[0], (B, S, H), dtype=jnp.float32)
        Wr = jax.random.normal(ks[1], (E, H), dtype=jnp.float32) * 0.02
        Wi = jax.random.normal(ks[2], (E, F, H), dtype=jnp.float32) * 0.02
        bi = jnp.zeros((E, F), dtype=jnp.float32)
        Wo = jax.random.normal(ks[3], (E, H, F), dtype=jnp.float32) * 0.02
        bo = jnp.zeros((E, H), dtype=jnp.float32)
        return {'x': x, 'Wr': Wr, 'Wi': Wi, 'bi': bi, 'Wo': Wo, 'bo': bo}
    _L0_ffn_all = _L0_ffn_setup()
    _L0_ffn_in = {k: v for k, v in _L0_ffn_all.items() if k in ('Wr', 'Wi', 'bi', 'Wo', 'bo')}
    del _L0_ffn_all

    def _L1_attn_setup():
        import jax, jax.numpy as jnp
        import numpy as np
        import math
        D_MODEL, N_HEADS, D_HEAD = (192, 12, 64)
        INIT_RANGE = 0.02
        ROPE_BASE = 10000.0

        def _rope_cos_sin(seq_len, d_head, dtype=jnp.float32):
            inv_freq = 1.0 / ROPE_BASE ** (jnp.arange(0, d_head, 2, dtype=jnp.float32) / d_head)
            ang = jnp.arange(seq_len, dtype=jnp.float32)[:, None] * inv_freq[None, :]
            return (jnp.cos(ang).astype(dtype), jnp.sin(ang).astype(dtype))

        def _apply_rope(x, cos, sin):
            xr, xi = (x[..., 0::2], x[..., 1::2])
            c = cos[None, :, None, :]
            s = sin[None, :, None, :]
            out_r = xr * c - xi * s
            out_i = xr * s + xi * c
            return jnp.stack([out_r, out_i], axis=-1).reshape(x.shape)
        key = jax.random.key(seed)
        ks = jax.random.split(key, 5)
        B, T = (2, 512)
        x = jax.random.normal(ks[0], (B, T, D_MODEL), dtype=jnp.float32)
        W_Q = INIT_RANGE * jax.random.normal(ks[1], (N_HEADS, D_MODEL, D_HEAD), dtype=jnp.float32)
        W_K = INIT_RANGE * jax.random.normal(ks[2], (N_HEADS, D_MODEL, D_HEAD), dtype=jnp.float32)
        W_V = INIT_RANGE * jax.random.normal(ks[3], (N_HEADS, D_MODEL, D_HEAD), dtype=jnp.float32)
        W_O = INIT_RANGE * jax.random.normal(ks[4], (N_HEADS, D_HEAD, D_MODEL), dtype=jnp.float32)
        b_Q = jnp.zeros((N_HEADS, D_HEAD), dtype=jnp.float32)
        b_K = jnp.zeros((N_HEADS, D_HEAD), dtype=jnp.float32)
        b_V = jnp.zeros((N_HEADS, D_HEAD), dtype=jnp.float32)
        b_O = jnp.zeros((D_MODEL,), dtype=jnp.float32)
        return {'normalized_resid_pre': x, 'W_Q': W_Q, 'b_Q': b_Q, 'W_K': W_K, 'b_K': b_K, 'W_V': W_V, 'b_V': b_V, 'W_O': W_O, 'b_O': b_O}
    _L1_attn_all = _L1_attn_setup()
    _L1_attn_in = {k: v for k, v in _L1_attn_all.items() if k in ('W_Q', 'b_Q', 'W_K', 'b_K', 'W_V', 'b_V', 'W_O', 'b_O')}
    del _L1_attn_all

    def _L1_ffn_setup():
        import math
        import jax, jax.numpy as jnp
        import numpy as np
        B, L, D = (8, 1024, 192)
        E = 16
        TOP_K = 2
        F_EXP = 4 * D
        F_SH = F_EXP * 2 // 4
        key = jax.random.key(seed)
        ks = jax.random.split(key, 8)
        s = lambda fan_in: 1.0 / math.sqrt(fan_in)
        return {'hidden_states': jax.random.normal(ks[0], (B, L, D), jnp.float32), 'gate_weight': jax.random.uniform(ks[1], (E, D), jnp.float32, -s(D), s(D)), 'Wg': jax.random.uniform(ks[2], (E, F_EXP, D), jnp.float32, -s(D), s(D)), 'Wu': jax.random.uniform(ks[3], (E, F_EXP, D), jnp.float32, -s(D), s(D)), 'Wd': jax.random.uniform(ks[4], (E, D, F_EXP), jnp.float32, -s(F_EXP), s(F_EXP)), 'Ws_g': jax.random.uniform(ks[5], (F_SH, D), jnp.float32, -s(D), s(D)), 'Ws_u': jax.random.uniform(ks[6], (F_SH, D), jnp.float32, -s(D), s(D)), 'Ws_d': jax.random.uniform(ks[7], (D, F_SH), jnp.float32, -s(F_SH), s(F_SH))}
    _L1_ffn_all = _L1_ffn_setup()
    _L1_ffn_in = {k: v for k, v in _L1_ffn_all.items() if k in ('gate_weight', 'Wg', 'Wu', 'Wd', 'Ws_g', 'Ws_u', 'Ws_d')}
    del _L1_ffn_all

    def _L2_attn_setup():
        import jax, jax.numpy as jnp
        import numpy as np
        NUM_HEADS = 12
        NUM_LANDMARKS = 64
        DIM = 192

        def _iterative_inv(mat, n_iter=6):
            L = mat.shape[-1]
            I = jnp.eye(L, dtype=mat.dtype)
            K = mat
            denom = jnp.max(jnp.sum(K, axis=-2), axis=-1)[:, :, None, None]
            V = 1.0 / denom * jnp.swapaxes(K, -1, -2)
            for _ in range(n_iter):
                KV = jnp.matmul(K, V)
                V = jnp.matmul(0.25 * V, 13.0 * I - jnp.matmul(KV, 15.0 * I - jnp.matmul(KV, 7.0 * I - KV)))
            return V
        key = jax.random.key(seed)
        k1, k2, k3, k4 = jax.random.split(key, 4)
        B, N, C = (4, 1024, DIM)
        x = jax.random.normal(k1, (B, N, C), dtype=jnp.float32)
        w_qkv = jax.random.normal(k2, (3 * C, C), dtype=jnp.float32) * C ** (-0.5)
        w_proj = jax.random.normal(k3, (C, C), dtype=jnp.float32) * C ** (-0.5)
        b_proj = jax.random.normal(k4, (C,), dtype=jnp.float32) * 0.01
        return {'x': x, 'w_qkv': w_qkv, 'w_proj': w_proj, 'b_proj': b_proj}
    _L2_attn_all = _L2_attn_setup()
    _L2_attn_in = {k: v for k, v in _L2_attn_all.items() if k in ('w_qkv', 'w_proj', 'b_proj')}
    del _L2_attn_all

    def _L2_ffn_setup():
        import jax, jax.numpy as jnp
        import numpy as np
        GT0 = [[0, 1, 0, 0, 1, 0], [0, 1, 0, 0, 0, 1], [0, 0, 1, 0, 1, 0], [0, 0, 1, 0, 0, 1], [0, 0, 0, 1, 1, 0], [0, 0, 0, 1, 0, 1]]
        NCLS = 6
        K = 1

        def _expert_pairs():
            pairs = []
            for i in range(NCLS):
                p = [(j - 1, k - 1) for j in range(1, 6) for k in range(1, 6) if j != k and GT0[i][j] == 1 and (GT0[i][k] == 1)]
                pairs.append(p)
            return pairs
        PAIRS = _expert_pairs()
        B, P, D, H = (64, 64, 192, 768)

        def _gelu(t):
            return jax.nn.gelu(t, approximate=False)
        key = jax.random.key(seed)
        ks = jax.random.split(key, 8)
        s = 0.02
        x = jax.random.normal(ks[0], (B, NCLS + P, D), dtype=jnp.float32)
        mids = jax.random.randint(ks[1], (B,), 0, 6)
        moe0_W1 = jax.random.normal(ks[2], (D, H), dtype=jnp.float32) * s
        moe0_b1 = jnp.zeros((H,), jnp.float32)
        moe0_W2 = jax.random.normal(ks[3], (H, D), dtype=jnp.float32) * s
        moe0_b2 = jnp.zeros((D,), jnp.float32)
        A1_W = jax.random.normal(ks[4], (5, D, H), dtype=jnp.float32) * s
        A1_b = jnp.zeros((5, H), jnp.float32)
        A2_W = jax.random.normal(ks[5], (5, H, D), dtype=jnp.float32) * s
        A2_b = jnp.zeros((5, D), jnp.float32)
        G_W = jax.random.normal(ks[6], (NCLS, D, 2), dtype=jnp.float32) * s
        return {'x': x, 'moe0_W1': moe0_W1, 'moe0_b1': moe0_b1, 'moe0_W2': moe0_W2, 'moe0_b2': moe0_b2, 'A1_W': A1_W, 'A1_b': A1_b, 'A2_W': A2_W, 'A2_b': A2_b, 'G_W': G_W, 'mids': mids}
    _L2_ffn_all = _L2_ffn_setup()
    _L2_ffn_in = {k: v for k, v in _L2_ffn_all.items() if k in ('moe0_W1', 'moe0_b1', 'moe0_W2', 'moe0_b2', 'A1_W', 'A1_b', 'A2_W', 'A2_b', 'G_W', 'mids')}
    del _L2_ffn_all

    def _L3_attn_setup():
        import jax, jax.numpy as jnp
        import numpy as np
        D_MODEL = 192
        D_STATE = 16
        D_CONV = 4
        EXPAND = 2
        D_INNER = EXPAND * D_MODEL
        DT_RANK = (D_MODEL + 15) // 16
        BATCH = 2
        SEQLEN = 256

        def _mamba(x, in_w, conv_w, conv_b, xproj_w, dt_w, dt_b, A_log, Dp, out_w):
            B, L, _ = x.shape
            xz = x @ in_w.T
            xc, z = jnp.split(xz, 2, axis=-1)
            K = conv_w.shape[1]
            xpad = jnp.pad(xc, ((0, 0), (K - 1, 0), (0, 0)))
            xconv = conv_b + sum((conv_w[:, k] * xpad[:, k:k + L, :] for k in range(K)))
            u = jax.nn.silu(xconv)
            proj = u @ xproj_w.T
            dt_rank = dt_w.shape[1]
            n = A_log.shape[1]
            dtx, Bm, Cm = jnp.split(proj, [dt_rank, dt_rank + n], axis=-1)
            dt = jax.nn.softplus(dtx @ dt_w.T + dt_b)
            A = -jnp.exp(A_log)
            dA = jnp.exp(dt[..., None] * A)
            dBu = dt[..., None] * Bm[:, :, None, :] * u[..., None]

            def step(h, inp):
                dA_t, dBu_t, C_t = inp
                h = dA_t * h + dBu_t
                y = jnp.einsum('bdn,bn->bd', h, C_t)
                return (h, y)
            h0 = jnp.zeros((B, u.shape[-1], n), x.dtype)
            _, ys = jax.lax.scan(step, h0, (dA.transpose(1, 0, 2, 3), dBu.transpose(1, 0, 2, 3), Cm.transpose(1, 0, 2)))
            y = ys.transpose(1, 0, 2) + u * Dp
            y = y * jax.nn.silu(z)
            return y @ out_w.T
        key = jax.random.key(seed)
        ks = jax.random.split(key, 10)
        s = 0.02
        f32 = jnp.float32
        x = jax.random.normal(ks[0], (BATCH, SEQLEN, D_MODEL), f32)
        bm_in_w = jax.random.normal(ks[1], (2 * D_MODEL, D_MODEL), f32) * s
        bm_in_b = jnp.zeros((2 * D_MODEL,), f32)
        bm_out_w = jax.random.normal(ks[2], (D_MODEL, D_MODEL), f32) * s
        bm_out_b = jnp.zeros((D_MODEL,), f32)
        m_in_w = jax.random.normal(ks[3], (2 * D_INNER, D_MODEL), f32) * s
        m_conv_w = jax.random.normal(ks[4], (D_INNER, D_CONV), f32) * s
        m_conv_b = jnp.zeros((D_INNER,), f32)
        m_xproj_w = jax.random.normal(ks[5], (DT_RANK + 2 * D_STATE, D_INNER), f32) * s
        m_dt_w = jax.random.normal(ks[6], (D_INNER, DT_RANK), f32) * s
        m_dt_b = jnp.full((D_INNER,), -4.6, f32)
        m_A_log = jnp.log(jnp.broadcast_to(jnp.arange(1, D_STATE + 1, dtype=f32), (D_INNER, D_STATE)))
        m_D = jnp.ones((D_INNER,), f32)
        m_out_w = jax.random.normal(ks[7], (D_MODEL, D_INNER), f32) * s
        ln_g = jnp.ones((D_MODEL,), f32)
        ln_b = jnp.zeros((D_MODEL,), f32)
        return {'x': x, 'bm_in_w': bm_in_w, 'bm_in_b': bm_in_b, 'bm_out_w': bm_out_w, 'bm_out_b': bm_out_b, 'm_in_w': m_in_w, 'm_conv_w': m_conv_w, 'm_conv_b': m_conv_b, 'm_xproj_w': m_xproj_w, 'm_dt_w': m_dt_w, 'm_dt_b': m_dt_b, 'm_A_log': m_A_log, 'm_D': m_D, 'm_out_w': m_out_w, 'ln_g': ln_g, 'ln_b': ln_b}
    _L3_attn_all = _L3_attn_setup()
    _L3_attn_in = {k: v for k, v in _L3_attn_all.items() if k in ('bm_in_w', 'bm_in_b', 'bm_out_w', 'bm_out_b', 'm_in_w', 'm_conv_w', 'm_conv_b', 'm_xproj_w', 'm_dt_w', 'm_dt_b', 'm_A_log', 'm_D', 'm_out_w', 'ln_g', 'ln_b')}
    del _L3_attn_all

    def _L3_ffn_setup():
        import jax, jax.numpy as jnp
        import numpy as np
        S, B, DIM = (256, 4, 192)
        N_EXPERTS = 8
        HID = 512
        key = jax.random.key(seed)
        ks = jax.random.split(key, 6)
        scale = 0.02
        return {'hidden_states': jax.random.normal(ks[0], (S, B, DIM), dtype=jnp.float32), 'router_w': jax.random.normal(ks[1], (DIM, N_EXPERTS), dtype=jnp.float32) * scale, 'router_b': jnp.zeros((N_EXPERTS,), dtype=jnp.float32), 'w1': jax.random.normal(ks[2], (N_EXPERTS, DIM, HID), dtype=jnp.float32) * scale, 'w2': jax.random.normal(ks[3], (N_EXPERTS, DIM, HID), dtype=jnp.float32) * scale, 'w3': jax.random.normal(ks[4], (N_EXPERTS, HID, DIM), dtype=jnp.float32) * scale}
    _L3_ffn_all = _L3_ffn_setup()
    _L3_ffn_in = {k: v for k, v in _L3_ffn_all.items() if k in ('router_w', 'router_b', 'w1', 'w2', 'w3')}
    del _L3_ffn_all
    return {'x': x, 'L0_tok_ln_scale': _L0_tok_in['ln_scale'], 'L0_tok_W': _L0_tok_in['W'], 'L0_tok_b': _L0_tok_in['b'], 'L0_attn_qkv_w': _L0_attn_in['qkv_w'], 'L0_attn_qkv_b': _L0_attn_in['qkv_b'], 'L0_attn_qkv_B': _L0_attn_in['qkv_B'], 'L0_attn_proj_w': _L0_attn_in['proj_w'], 'L0_attn_proj_b': _L0_attn_in['proj_b'], 'L0_attn_proj_B': _L0_attn_in['proj_B'], 'L0_ffn_Wr': _L0_ffn_in['Wr'], 'L0_ffn_Wi': _L0_ffn_in['Wi'], 'L0_ffn_bi': _L0_ffn_in['bi'], 'L0_ffn_Wo': _L0_ffn_in['Wo'], 'L0_ffn_bo': _L0_ffn_in['bo'], 'L1_attn_W_Q': _L1_attn_in['W_Q'], 'L1_attn_b_Q': _L1_attn_in['b_Q'], 'L1_attn_W_K': _L1_attn_in['W_K'], 'L1_attn_b_K': _L1_attn_in['b_K'], 'L1_attn_W_V': _L1_attn_in['W_V'], 'L1_attn_b_V': _L1_attn_in['b_V'], 'L1_attn_W_O': _L1_attn_in['W_O'], 'L1_attn_b_O': _L1_attn_in['b_O'], 'L1_ffn_gate_weight': _L1_ffn_in['gate_weight'], 'L1_ffn_Wg': _L1_ffn_in['Wg'], 'L1_ffn_Wu': _L1_ffn_in['Wu'], 'L1_ffn_Wd': _L1_ffn_in['Wd'], 'L1_ffn_Ws_g': _L1_ffn_in['Ws_g'], 'L1_ffn_Ws_u': _L1_ffn_in['Ws_u'], 'L1_ffn_Ws_d': _L1_ffn_in['Ws_d'], 'L2_attn_w_qkv': _L2_attn_in['w_qkv'], 'L2_attn_w_proj': _L2_attn_in['w_proj'], 'L2_attn_b_proj': _L2_attn_in['b_proj'], 'L2_ffn_moe0_W1': _L2_ffn_in['moe0_W1'], 'L2_ffn_moe0_b1': _L2_ffn_in['moe0_b1'], 'L2_ffn_moe0_W2': _L2_ffn_in['moe0_W2'], 'L2_ffn_moe0_b2': _L2_ffn_in['moe0_b2'], 'L2_ffn_A1_W': _L2_ffn_in['A1_W'], 'L2_ffn_A1_b': _L2_ffn_in['A1_b'], 'L2_ffn_A2_W': _L2_ffn_in['A2_W'], 'L2_ffn_A2_b': _L2_ffn_in['A2_b'], 'L2_ffn_G_W': _L2_ffn_in['G_W'], 'L2_ffn_mids': _L2_ffn_in['mids'], 'L3_attn_bm_in_w': _L3_attn_in['bm_in_w'], 'L3_attn_bm_in_b': _L3_attn_in['bm_in_b'], 'L3_attn_bm_out_w': _L3_attn_in['bm_out_w'], 'L3_attn_bm_out_b': _L3_attn_in['bm_out_b'], 'L3_attn_m_in_w': _L3_attn_in['m_in_w'], 'L3_attn_m_conv_w': _L3_attn_in['m_conv_w'], 'L3_attn_m_conv_b': _L3_attn_in['m_conv_b'], 'L3_attn_m_xproj_w': _L3_attn_in['m_xproj_w'], 'L3_attn_m_dt_w': _L3_attn_in['m_dt_w'], 'L3_attn_m_dt_b': _L3_attn_in['m_dt_b'], 'L3_attn_m_A_log': _L3_attn_in['m_A_log'], 'L3_attn_m_D': _L3_attn_in['m_D'], 'L3_attn_m_out_w': _L3_attn_in['m_out_w'], 'L3_attn_ln_g': _L3_attn_in['ln_g'], 'L3_attn_ln_b': _L3_attn_in['ln_b'], 'L3_ffn_router_w': _L3_ffn_in['router_w'], 'L3_ffn_router_b': _L3_ffn_in['router_b'], 'L3_ffn_w1': _L3_ffn_in['w1'], 'L3_ffn_w2': _L3_ffn_in['w2'], 'L3_ffn_w3': _L3_ffn_in['w3']}

def reference(x, L0_tok_ln_scale, L0_tok_W, L0_tok_b, L0_attn_qkv_w, L0_attn_qkv_b, L0_attn_qkv_B, L0_attn_proj_w, L0_attn_proj_b, L0_attn_proj_B, L0_ffn_Wr, L0_ffn_Wi, L0_ffn_bi, L0_ffn_Wo, L0_ffn_bo, L1_attn_W_Q, L1_attn_b_Q, L1_attn_W_K, L1_attn_b_K, L1_attn_W_V, L1_attn_b_V, L1_attn_W_O, L1_attn_b_O, L1_ffn_gate_weight, L1_ffn_Wg, L1_ffn_Wu, L1_ffn_Wd, L1_ffn_Ws_g, L1_ffn_Ws_u, L1_ffn_Ws_d, L2_attn_w_qkv, L2_attn_w_proj, L2_attn_b_proj, L2_ffn_moe0_W1, L2_ffn_moe0_b1, L2_ffn_moe0_W2, L2_ffn_moe0_b2, L2_ffn_A1_W, L2_ffn_A1_b, L2_ffn_A2_W, L2_ffn_A2_b, L2_ffn_G_W, L2_ffn_mids, L3_attn_bm_in_w, L3_attn_bm_in_b, L3_attn_bm_out_w, L3_attn_bm_out_b, L3_attn_m_in_w, L3_attn_m_conv_w, L3_attn_m_conv_b, L3_attn_m_xproj_w, L3_attn_m_dt_w, L3_attn_m_dt_b, L3_attn_m_A_log, L3_attn_m_D, L3_attn_m_out_w, L3_attn_ln_g, L3_attn_ln_b, L3_ffn_router_w, L3_ffn_router_b, L3_ffn_w1, L3_ffn_w2, L3_ffn_w3):
    import jax
    import jax.numpy as jnp

    def _L0_tok_ref(x, ln_scale, W, b):
        import jax, jax.numpy as jnp
        import numpy as np
        PATCH = 16
        EPS = 1e-05

        def _shifts(x):
            b, h, w, c = x.shape
            zc = jnp.zeros((b, h, 1, c), x.dtype)
            zr = jnp.zeros((b, 1, w, c), x.dtype)
            s_right = jnp.concatenate([zc, x[:, :, :-1, :]], axis=2)
            s_left = jnp.concatenate([x[:, :, 1:, :], zc], axis=2)
            s_down = jnp.concatenate([zr, x[:, :-1, :, :]], axis=1)
            s_up = jnp.concatenate([x[:, 1:, :, :], zr], axis=1)
            return [s_right, s_left, s_down, s_up]
        bsz, H, Wd, c = x.shape
        xs = jnp.concatenate([x] + _shifts(x), axis=-1)
        c5 = 5 * c
        hp, wp = (H // PATCH, Wd // PATCH)
        xs = xs.reshape(bsz, hp, PATCH, wp, PATCH, c5)
        xs = xs.transpose(0, 1, 3, 2, 4, 5).reshape(bsz, hp * wp, PATCH * PATCH * c5)
        mu = jnp.mean(xs, axis=-1, keepdims=True)
        var = jnp.mean(jnp.square(xs - mu), axis=-1, keepdims=True)
        xn = (xs - mu) * jax.lax.rsqrt(var + EPS) * ln_scale
        return jnp.einsum('btf,fd->btd', xn, W) + b

    def _L0_attn_ref(x, qkv_w, qkv_b, qkv_B, proj_w, proj_b, proj_B):
        import jax, jax.numpy as jnp
        import numpy as np
        import math
        DIM = 192
        NUM_HEADS = 12

        def _xavier_uniform(key, out_f, in_f):
            a = math.sqrt(6.0 / (in_f + out_f))
            return jax.random.uniform(key, (out_f, in_f), jnp.float32, -a, a)
        B, N, C = x.shape
        hd = C // NUM_HEADS
        scale = hd ** (-0.5)
        qkv = x @ qkv_w.T + qkv_b
        qkv = qkv.reshape(B, N, 3, NUM_HEADS, hd).transpose(2, 0, 3, 1, 4)
        q, k, v = (qkv[0], qkv[1], qkv[2])
        attn = jnp.einsum('bhnd,bhmd->bhnm', q, k) * scale
        attn = jax.nn.softmax(attn, axis=-1)
        out = jnp.einsum('bhnm,bhmd->bhnd', attn, v)
        out = out.transpose(0, 2, 1, 3).reshape(B, N, C)
        return out @ proj_w.T + proj_b

    def _L0_ffn_ref(x, Wr, Wi, bi, Wo, bo):
        import jax, jax.numpy as jnp
        import numpy as np
        B, S, H, F, E, TOP_K = (4, 512, 192, 768, 8, 2)
        xf = x.reshape(-1, x.shape[-1])
        router_logits = jnp.einsum('th,eh->te', xf, Wr)
        topk_vals, topk_idx = jax.lax.top_k(router_logits, TOP_K)
        routing_weights = jax.nn.softmax(topk_vals, axis=-1)
        h = jnp.einsum('th,efh->etf', xf, Wi) + bi[:, None, :]
        h = jax.nn.gelu(h, approximate=False)
        expert_out = jnp.einsum('etf,ehf->eth', h, Wo) + bo[:, None, :]
        expert_out = jnp.transpose(expert_out, (1, 0, 2))
        gathered = jnp.take_along_axis(expert_out, topk_idx[:, :, None], axis=1)
        out = jnp.einsum('tk,tkh->th', routing_weights, gathered)
        return out.reshape(x.shape)

    def _L1_attn_ref(normalized_resid_pre, W_Q, b_Q, W_K, b_K, W_V, b_V, W_O, b_O):
        import jax, jax.numpy as jnp
        import numpy as np
        import math
        D_MODEL, N_HEADS, D_HEAD = (192, 12, 64)
        INIT_RANGE = 0.02
        ROPE_BASE = 10000.0

        def _rope_cos_sin(seq_len, d_head, dtype=jnp.float32):
            inv_freq = 1.0 / ROPE_BASE ** (jnp.arange(0, d_head, 2, dtype=jnp.float32) / d_head)
            ang = jnp.arange(seq_len, dtype=jnp.float32)[:, None] * inv_freq[None, :]
            return (jnp.cos(ang).astype(dtype), jnp.sin(ang).astype(dtype))

        def _apply_rope(x, cos, sin):
            xr, xi = (x[..., 0::2], x[..., 1::2])
            c = cos[None, :, None, :]
            s = sin[None, :, None, :]
            out_r = xr * c - xi * s
            out_i = xr * s + xi * c
            return jnp.stack([out_r, out_i], axis=-1).reshape(x.shape)
        x = normalized_resid_pre
        B, T, _ = x.shape
        cos, sin = _rope_cos_sin(T, D_HEAD, x.dtype)
        Q = jnp.einsum('btc,hcd->bthd', x, W_Q) + b_Q
        K = jnp.einsum('btc,hcd->bthd', x, W_K) + b_K
        V = jnp.einsum('btc,hcd->bthd', x, W_V) + b_V
        Q = _apply_rope(Q, cos, sin)
        K = _apply_rope(K, cos, sin)
        scores = jnp.einsum('bqhd,bkhd->bhqk', Q, K) / math.sqrt(D_HEAD)
        tril = jnp.tril(jnp.ones((T, T), dtype=bool))
        z = jnp.where(tril[None, None], scores, 0.0)
        z = jnp.where(z == 0.0, -jnp.inf, z)
        probs = jax.nn.softmax(z, axis=-1)
        o = jnp.einsum('bhqk,bkhd->bqhd', probs, V)
        return jnp.einsum('bqhd,hdm->bqm', o, W_O) + b_O

    def _L1_ffn_ref(hidden_states, gate_weight, Wg, Wu, Wd, Ws_g, Ws_u, Ws_d):
        import math
        import jax, jax.numpy as jnp
        import numpy as np
        B, L, D = (8, 1024, 192)
        E = 16
        TOP_K = 2
        F_EXP = 4 * D
        F_SH = F_EXP * 2 // 4
        b, l, d = hidden_states.shape
        n = b * l
        x = hidden_states.reshape(n, d)
        scores = jax.nn.sigmoid(x @ gate_weight.T)
        capacity = math.ceil(n / E * TOP_K)
        topk_score, topk_ids = jax.lax.top_k(scores.T, capacity)
        xg = x[topk_ids]
        gate = jax.nn.silu(jnp.einsum('ecd,efd->ecf', xg, Wg))
        up = jnp.einsum('ecd,efd->ecf', xg, Wu)
        out = jnp.einsum('ecf,edf->ecd', gate * up, Wd)
        out = out * topk_score[..., None]
        y = jnp.zeros((n, d), x.dtype).at[topk_ids.reshape(-1)].add(out.reshape(-1, d))
        y = y.reshape(b, l, d)
        shared = jax.nn.silu(hidden_states @ Ws_g.T) * (hidden_states @ Ws_u.T) @ Ws_d.T
        return y + shared

    def _L2_attn_ref(x, w_qkv, w_proj, b_proj):
        import jax, jax.numpy as jnp
        import numpy as np
        NUM_HEADS = 12
        NUM_LANDMARKS = 64
        DIM = 192

        def _iterative_inv(mat, n_iter=6):
            L = mat.shape[-1]
            I = jnp.eye(L, dtype=mat.dtype)
            K = mat
            denom = jnp.max(jnp.sum(K, axis=-2), axis=-1)[:, :, None, None]
            V = 1.0 / denom * jnp.swapaxes(K, -1, -2)
            for _ in range(n_iter):
                KV = jnp.matmul(K, V)
                V = jnp.matmul(0.25 * V, 13.0 * I - jnp.matmul(KV, 15.0 * I - jnp.matmul(KV, 7.0 * I - KV)))
            return V
        B, N, C = x.shape
        H, Lm = (NUM_HEADS, NUM_LANDMARKS)
        hd = C // H
        scale = hd ** 0.5
        qkv = (x @ w_qkv.T).reshape(B, N, 3, H, hd).transpose(2, 0, 3, 1, 4)
        q, k, v = (qkv[0], qkv[1], qkv[2])
        q = q / scale
        segs = N // Lm
        keys_landmarks = k.reshape(B, H, Lm, segs, hd).mean(axis=-2)
        queries_landmarks = q.reshape(B, H, Lm, segs, hd).mean(axis=-2)
        kernel_1 = jax.nn.softmax(jnp.einsum('bhnd,bhld->bhnl', q, keys_landmarks), axis=-1)
        kernel_2 = jax.nn.softmax(jnp.einsum('bhmd,bhld->bhml', queries_landmarks, keys_landmarks), axis=-1)
        kernel_3 = jax.nn.softmax(jnp.einsum('bhld,bhnd->bhln', queries_landmarks, k), axis=-1)
        out = jnp.matmul(jnp.matmul(kernel_1, _iterative_inv(kernel_2)), jnp.matmul(kernel_3, v))
        out = out.transpose(0, 2, 1, 3).reshape(B, N, C)
        return out @ w_proj.T + b_proj

    def _L2_ffn_ref(x, moe0_W1, moe0_b1, moe0_W2, moe0_b2, A1_W, A1_b, A2_W, A2_b, G_W, mids):
        import jax, jax.numpy as jnp
        import numpy as np
        GT0 = [[0, 1, 0, 0, 1, 0], [0, 1, 0, 0, 0, 1], [0, 0, 1, 0, 1, 0], [0, 0, 1, 0, 0, 1], [0, 0, 0, 1, 1, 0], [0, 0, 0, 1, 0, 1]]
        NCLS = 6
        K = 1

        def _expert_pairs():
            pairs = []
            for i in range(NCLS):
                p = [(j - 1, k - 1) for j in range(1, 6) for k in range(1, 6) if j != k and GT0[i][j] == 1 and (GT0[i][k] == 1)]
                pairs.append(p)
            return pairs
        PAIRS = _expert_pairs()
        B, P, D, H = (64, 64, 192, 768)

        def _gelu(t):
            return jax.nn.gelu(t, approximate=False)
        cls_tokens = x[:, :NCLS]
        patch_tokens = x[:, NCLS:]
        patch_out = _gelu(patch_tokens @ moe0_W1 + moe0_b1) @ moe0_W2 + moe0_b2
        cls_outs = []
        for i in range(NCLS):
            tok = cls_tokens[:, i]
            eouts = [_gelu(tok @ A1_W[a] + A1_b[a]) @ A2_W[c] + A2_b[c] for a, c in PAIRS[i]]
            out = jnp.stack(eouts, axis=-1)
            gate = jax.nn.softmax(tok @ G_W[i], axis=-1)
            thr = jnp.sort(gate, axis=-1)[..., -(K + 1)]
            mask = (gate > thr[..., None]).astype(gate.dtype)
            g = gate * mask
            g = g / jnp.clip(jnp.sum(g, axis=-1, keepdims=True), 1e-06)
            cls_outs.append(jnp.sum(out * g[:, None, :], axis=-1))
        cls_out = jnp.stack(cls_outs, axis=1)
        return jnp.concatenate([cls_out, patch_out], axis=1)

    def _L3_attn_ref(x, bm_in_w, bm_in_b, bm_out_w, bm_out_b, m_in_w, m_conv_w, m_conv_b, m_xproj_w, m_dt_w, m_dt_b, m_A_log, m_D, m_out_w, ln_g, ln_b):
        import jax, jax.numpy as jnp
        import numpy as np
        D_MODEL = 192
        D_STATE = 16
        D_CONV = 4
        EXPAND = 2
        D_INNER = EXPAND * D_MODEL
        DT_RANK = (D_MODEL + 15) // 16
        BATCH = 2
        SEQLEN = 256

        def _mamba(x, in_w, conv_w, conv_b, xproj_w, dt_w, dt_b, A_log, Dp, out_w):
            B, L, _ = x.shape
            xz = x @ in_w.T
            xc, z = jnp.split(xz, 2, axis=-1)
            K = conv_w.shape[1]
            xpad = jnp.pad(xc, ((0, 0), (K - 1, 0), (0, 0)))
            xconv = conv_b + sum((conv_w[:, k] * xpad[:, k:k + L, :] for k in range(K)))
            u = jax.nn.silu(xconv)
            proj = u @ xproj_w.T
            dt_rank = dt_w.shape[1]
            n = A_log.shape[1]
            dtx, Bm, Cm = jnp.split(proj, [dt_rank, dt_rank + n], axis=-1)
            dt = jax.nn.softplus(dtx @ dt_w.T + dt_b)
            A = -jnp.exp(A_log)
            dA = jnp.exp(dt[..., None] * A)
            dBu = dt[..., None] * Bm[:, :, None, :] * u[..., None]

            def step(h, inp):
                dA_t, dBu_t, C_t = inp
                h = dA_t * h + dBu_t
                y = jnp.einsum('bdn,bn->bd', h, C_t)
                return (h, y)
            h0 = jnp.zeros((B, u.shape[-1], n), x.dtype)
            _, ys = jax.lax.scan(step, h0, (dA.transpose(1, 0, 2, 3), dBu.transpose(1, 0, 2, 3), Cm.transpose(1, 0, 2)))
            y = ys.transpose(1, 0, 2) + u * Dp
            y = y * jax.nn.silu(z)
            return y @ out_w.T
        mparams = (m_in_w, m_conv_w, m_conv_b, m_xproj_w, m_dt_w, m_dt_b, m_A_log, m_D, m_out_w)
        xp = x @ bm_in_w.T + bm_in_b
        x_f, x_b = jnp.split(xp, 2, axis=-1)
        out_f = _mamba(x_f, *mparams)
        out_b = jnp.flip(_mamba(jnp.flip(x_b, axis=1), *mparams), axis=1)
        mo = (out_f + out_b) @ bm_out_w.T + bm_out_b
        h = mo + x
        mu = jnp.mean(h, axis=-1, keepdims=True)
        var = jnp.mean(jnp.square(h - mu), axis=-1, keepdims=True)
        return (h - mu) * jax.lax.rsqrt(var + 1e-05) * ln_g + ln_b

    def _L3_ffn_ref(hidden_states, router_w, router_b, w1, w2, w3):
        import jax, jax.numpy as jnp
        import numpy as np
        S, B, DIM = (256, 4, 192)
        N_EXPERTS = 8
        HID = 512
        s, b, h = hidden_states.shape
        route = jax.nn.softmax(hidden_states @ router_w + router_b, axis=2)
        max_prob = jnp.max(route, axis=2).reshape(-1, 1)
        max_ind = jnp.argmax(route, axis=2).reshape(-1)
        x = hidden_states.reshape(-1, h)
        out = jnp.zeros_like(x)
        for e in range(N_EXPERTS):
            mask = (max_ind == e)[:, None]
            xe = jnp.where(mask, x, 0.0)
            oe = jax.nn.silu(xe @ w1[e]) * (xe @ w2[e]) @ w3[e]
            out = out + jnp.where(mask, oe, 0.0)
        out = out.astype(jnp.bfloat16) * max_prob
        return out.reshape(s, b, h)
    h = _L0_tok_ref(x, L0_tok_ln_scale, L0_tok_W, L0_tok_b)
    h = h + _L0_attn_ref(_layernorm(h, axis=-1), L0_attn_qkv_w, L0_attn_qkv_b, L0_attn_qkv_B, L0_attn_proj_w, L0_attn_proj_b, L0_attn_proj_B)
    h = h + _L0_ffn_ref(_layernorm(h, axis=-1), L0_ffn_Wr, L0_ffn_Wi, L0_ffn_bi, L0_ffn_Wo, L0_ffn_bo)
    h = h + _L1_attn_ref(_layernorm(h, axis=-1), L1_attn_W_Q, L1_attn_b_Q, L1_attn_W_K, L1_attn_b_K, L1_attn_W_V, L1_attn_b_V, L1_attn_W_O, L1_attn_b_O)
    h = h + _L1_ffn_ref(_layernorm(h, axis=-1), L1_ffn_gate_weight, L1_ffn_Wg, L1_ffn_Wu, L1_ffn_Wd, L1_ffn_Ws_g, L1_ffn_Ws_u, L1_ffn_Ws_d)
    h = h + _L2_attn_ref(_layernorm(h, axis=-1), L2_attn_w_qkv, L2_attn_w_proj, L2_attn_b_proj)
    h = h + _L2_ffn_ref(_layernorm(h, axis=-1), L2_ffn_moe0_W1, L2_ffn_moe0_b1, L2_ffn_moe0_W2, L2_ffn_moe0_b2, L2_ffn_A1_W, L2_ffn_A1_b, L2_ffn_A2_W, L2_ffn_A2_b, L2_ffn_G_W, L2_ffn_mids)
    h = h + _L3_attn_ref(_layernorm(h, axis=-1), L3_attn_bm_in_w, L3_attn_bm_in_b, L3_attn_bm_out_w, L3_attn_bm_out_b, L3_attn_m_in_w, L3_attn_m_conv_w, L3_attn_m_conv_b, L3_attn_m_xproj_w, L3_attn_m_dt_w, L3_attn_m_dt_b, L3_attn_m_A_log, L3_attn_m_D, L3_attn_m_out_w, L3_attn_ln_g, L3_attn_ln_b)
    h = h + _L3_ffn_ref(_layernorm(h, axis=-1), L3_ffn_router_w, L3_ffn_router_b, L3_ffn_w1, L3_ffn_w2, L3_ffn_w3)
    return h

_drawn_inputs = setup_inputs


def setup_inputs(seed=0):
    import zlib

    import numpy as np

    out = dict(_drawn_inputs(seed))
    spreads = {'L0_tok_ln_scale': (1.0, 0.2),
     'L0_tok_b': (0.0, 0.1),
     'L0_attn_qkv_b': (0.0, 0.1),
     'L0_attn_proj_b': (0.0, 0.1),
     'L0_ffn_bi': (0.0, 0.312),
     'L0_ffn_bo': (0.0, 0.1),
     'L1_attn_b_Q': (0.0, 0.8),
     'L1_attn_b_K': (0.0, 0.8),
     'L1_attn_b_V': (0.0, 0.1),
     'L1_attn_b_O': (0.0, 0.1),
     'L2_ffn_moe0_b1': (0.0, 0.321),
     'L2_ffn_moe0_b2': (0.0, 0.1),
     'L2_ffn_A1_b': (0.0, 0.8),
     'L2_ffn_A2_b': (0.0, 0.301),
     'L3_attn_bm_in_b': (0.0, 0.8),
     'L3_attn_bm_out_b': (0.0, 0.8),
     'L3_attn_m_conv_b': (0.0, 0.8),
     'L3_attn_m_dt_b': (-4.599999904632568, 0.6),
     'L3_attn_m_D': (1.0, 0.6),
     'L3_attn_ln_g': (1.0, 0.2),
     'L3_attn_ln_b': (0.0, 0.1),
     'L3_ffn_router_b': (0.0, 0.8)}
    factors = {'L1_attn_W_Q': 8.0,
     'L1_attn_W_K': 8.0,
     'L2_attn_b_proj': 6.731,
     'L3_attn_bm_in_w': 8.0,
     'L3_attn_bm_out_w': 8.0,
     'L3_attn_m_in_w': 8.0,
     'L3_attn_m_conv_w': 8.0,
     'L3_attn_m_xproj_w': 8.0,
     'L3_attn_m_dt_w': 8.0,
     'L3_attn_m_A_log': 8.0,
     'L3_attn_m_out_w': 8.0,
     'L3_ffn_router_w': 8.0,
     'L3_ffn_w1': 8.0,
     'L3_ffn_w2': 8.0,
     'L3_ffn_w3': 8.0}
    for name, (base, spread) in spreads.items():
        noise = np.random.default_rng([zlib.crc32(name.encode()), seed]).standard_normal(out[name].shape)
        drawn = base * np.exp(spread * noise) if base else spread * noise
        out[name] = jnp.asarray(drawn.astype(out[name].dtype))
    for name, factor in factors.items():
        out[name] = (out[name] * factor).astype(out[name].dtype)
    return out
```

```python
from collections import namedtuple
from contextlib import ExitStack, contextmanager

import numpy as np
import concourse.bass as bass
from concourse import mybir

F32 = mybir.dt.float32
BF16 = mybir.dt.bfloat16
U32 = mybir.dt.uint32
ALU = mybir.AluOpType
ACT = mybir.ActivationFunctionType
AX = mybir.AxisListType

P = 128
IMAGES, SIDE, CH = 32, 128, 3
PATCH = 16
GRID = SIDE // PATCH
SEQ = GRID * GRID
TOK = IMAGES * SEQ
TILES = TOK // P
D = 192
KC = 2
KP = D // KC
NB = 4
BLK = TOK // NB
HEADS = 12
EPS = 1e-5
SHIFTS = [(0, 0), (0, -1), (0, 1), (-1, 0), (1, 0)]
FEAT = PATCH * PATCH * len(SHIFTS) * CH
HALO = [(r, c) for r in range(-1, PATCH + 1) for c in range(-1, PATCH + 1)
        if not (r in (-1, PATCH) and c in (-1, PATCH))]
HF = len(HALO) * CH
HK = 8
HP = HF // HK
SLOTS = [4 * g + j for j in range(4) for g in range(3)]


class Resident:
    pass


@contextmanager
def phase(nc, tag, *names):
    sems = namedtuple("Sems", names)(*[nc.alloc_semaphore(f"{tag}_{n}") for n in names])
    with nc.Block() as block:
        yield block, sems
    nc.clear_and_free_semaphores(list(sems))
    nc.all_engine_barrier()


class Own:

    def __init__(self, eng, sem):
        self.eng, self.sem, self.n = eng, sem, 0

    def mark(self, ins):
        self.n += 1
        ins.then_inc(self.sem, 1)

    def settle(self):
        self.eng.wait_ge(self.sem, self.n)

    def link(self, ins):
        self.mark(ins)
        self.settle()


class Mem:

    def __init__(self, nc, tag):
        self.nc, self.tag, self.stack = nc, tag, ExitStack()

    def __enter__(self):
        self.stack.__enter__()
        return self

    def __exit__(self, *a):
        return self.stack.__exit__(*a)

    def sb(self, name, shape, dt=F32):
        return self.stack.enter_context(self.nc.sbuf_tensor(f"{self.tag}_{name}", shape, dt))

    def ps(self, name, shape, dt=F32):
        return self.stack.enter_context(self.nc.psum_tensor(f"{self.tag}_{name}", shape, dt))


def row(ap):
    return ap.rearrange("(a n) -> a n", a=1).partition_broadcast(P) if len(ap.shape) == 1 else ap



def constants(nc, R):
    with phase(nc, "const", "made") as (block, s):
        @block.gpsimd
        def _(pool):
            nc.gpsimd.memset(R.ident[:], 0.0).then_inc(s.made, 1)
            nc.gpsimd.memset(R.ones[:], 1.0)
            nc.gpsimd.memset(R.eps[:], EPS)
            pool.wait_ge(s.made, 1)
            nc.gpsimd.affine_select(out=R.ident[:], in_=R.ident[:], compare_op=ALU.not_equal, fill=1.0,
                                    base=0, pattern=[[-1, P]], channel_multiplier=1)



def tokenizer(nc, R, x, w, ln, mult, bias):
    with Mem(nc, "tok") as m:
        wsh = m.sb("wsh", [HP, HK, len(SHIFTS), D])
        lns = m.sb("lns", [HP, HK, len(SHIFTS)])
        weff = m.sb("weff", [HP, HK, D + 1])
        mul = m.sb("mul", [HP, HK])
        xt = m.sb("xt", [HP, 2, HK, P])
        sq = m.sb("sq", [HP, 2, HK, P])
        bb = m.sb("bb", [P, D])
        cs = m.sb("cs", [P, D])
        st = m.sb("st", [P, TILES, 8])
        raw = m.sb("raw", [P, TILES, D + 2])
        tmp = m.sb("tmp", [P, D])
        pA = m.ps("pA", [P, 512])
        pB = m.ps("pB", [P, 512])
        pQ = m.ps("pQ", [P, 512])
        pR = m.ps("pR", [P, 512])
        pC = m.ps("pC", [P, 512])
        out_ps, sq_ps = (pA, pB), (pQ, pR)
        with phase(nc, "tok", "w", "b", "x0", "x1", "weff", "sqd", "mm", "col", "raw", "v", "sd") as (block, s):
            @block.sync
            def _(sp):
                sp.dma_start(lns[:], ln).then_inc(s.w, 16)
                sp.dma_start(mul[:], mult).then_inc(s.w, 16)
                for k in range(HK):
                    sp.dma_start(wsh[:, k], w[:, k]).then_inc(s.w, 16)
                sp.dma_start(bb[:], row(bias)).then_inc(s.b, 16)
                with sp.Fori(0, TILES // 2) as i:
                    for u in range(2):
                        sp.wait_ge(s.mm, i * 2 + u + 1)
                        sp.dma_start(xt[:, u], x[i * 2 + u]).then_inc((s.x0, s.x1)[u], 16)

            @block.scalar
            def _(act):
                with act.Fori(0, TILES // 2) as i:
                    for u in range(2):
                        act.wait_ge((s.x0, s.x1)[u], i * 16 + 16)
                        act.wait_ge(s.mm, i * 2 + u + 1)
                        nc.scalar.activation(sq[:, u], xt[:, u], ACT.Square).then_inc(s.sqd, 1)
                act.wait_ge(s.v, 3)
                nc.scalar.activation(st[:, :, 2], st[:, :, 1], ACT.Sqrt, bias=R.eps[:]).then_inc(s.sd, 1)

            @block.tensor
            def _(pe):
                pe.wait_ge(s.weff, 1)
                for k in range(HK):
                    last = nc.tensor.matmul(pC[:, 0:D], R.ones[0:HP, :], weff[:, k, 0:D],
                                            start=(k == 0), stop=(k == HK - 1))
                last.then_inc(s.col, 1)
                nc.tensor.sem_inc(s.mm, 2)
                with pe.Fori(0, TILES // 2) as i:
                    for u in range(2):
                        pe.wait_ge((s.x0, s.x1)[u], i * 16 + 16)
                        pe.wait_ge(s.raw, i * 2 + u + 1)
                        pe.wait_ge(s.sqd, i * 2 + u + 1)
                        for k in range(HK):
                            nc.tensor.matmul(out_ps[u][:, 0:D + 1], xt[:, u, k], weff[:, k],
                                             start=(k == 0), stop=(k == HK - 1))
                        for k in range(HK):
                            last = nc.tensor.matmul(sq_ps[u][:, 0:1], sq[:, u, k], mul[:, k:k + 1],
                                                    start=(k == 0), stop=(k == HK - 1))
                        last.then_inc(s.mm, 1)

            @block.vector
            def _(dve):
                dve.wait_ge(s.w, 16 * (2 + HK))
                nc.vector.sem_inc(s.raw, 2)
                own = Own(dve, s.v)
                nc.vector.tensor_copy(weff[:, :, D], mul[:])
                n = 0
                for j in range(len(SHIFTS)):
                    for k in range(HK):
                        sc = lns[:, k, j:j + 1]
                        if j == 0:
                            ins = nc.vector.tensor_scalar(weff[:, k, 0:D], wsh[:, k, j], sc, None, ALU.mult)
                        else:
                            ins = nc.vector.scalar_tensor_tensor(weff[:, k, 0:D], wsh[:, k, j], sc,
                                                                 weff[:, k, 0:D], ALU.mult, ALU.add)
                    n += 1
                    if j < len(SHIFTS) - 1:
                        ins.then_inc(s.sd, 1)
                        dve.wait_ge(s.sd, n)
                    else:
                        ins.then_inc(s.weff, 1)
                dve.wait_ge(s.col, 1)
                nc.vector.tensor_copy(cs[:], pC[:, 0:D])
                with dve.Fori(0, TILES // 2) as i:
                    for u in range(2):
                        dve.wait_ge(s.mm, i * 2 + u + 3)
                        nc.vector.tensor_copy(raw[:, i * 2 + u, D + 1:D + 2], sq_ps[u][:, 0:1])
                        nc.vector.tensor_copy(raw[:, i * 2 + u, 0:D + 1], out_ps[u][:, 0:D + 1]).then_inc(s.raw, 1)
                dve.wait_ge(s.raw, TILES + 2)
                own.link(nc.vector.tensor_scalar(st[:, :, 0], raw[:, :, D], 1.0 / FEAT, None, ALU.mult))
                own.link(nc.vector.tensor_tensor(st[:, :, 3], st[:, :, 0], st[:, :, 0], ALU.mult))
                own.link(nc.vector.scalar_tensor_tensor(st[:, :, 1], raw[:, :, D + 1], 1.0 / FEAT, st[:, :, 3],
                                                        ALU.mult, ALU.subtract))
                dve.wait_ge(s.sd, len(SHIFTS))
                own.mark(nc.vector.reciprocal(st[:, :, 4], st[:, :, 2]))
                own.link(nc.vector.tensor_scalar(st[:, :, 5], st[:, :, 0], -1.0, None, ALU.mult))
                dve.wait_ge(s.b, 16)
                with dve.Fori(0, TILES) as t:
                    nc.vector.scalar_tensor_tensor(raw[:, t, 0:D], cs[:], st[:, t, 5:6], raw[:, t, 0:D],
                                                   ALU.mult, ALU.add).then_inc(s.v, 1)
                dve.wait_ge(s.v, own.n + TILES)
                with dve.Fori(0, TILES) as t:
                    nc.vector.scalar_tensor_tensor(R.h[:, t], raw[:, t, 0:D], st[:, t, 4:5], bb[:],
                                                   ALU.mult, ALU.add)



def normalise(nc, R, tag):
    with Mem(nc, tag) as m:
        st = m.sb("st", [P, TILES, nc.vector.BN_STATS_DIM])
        mv = m.sb("mv", [P, TILES, nc.vector.BN_AGGR_DIM])
        sd = m.sb("sd", [P, TILES])
        rs = m.sb("rs", [P, TILES])
        ps = [m.ps(f"t{k}", [P, 512]) for k in range(8)]
        with phase(nc, tag, "st", "mv", "sd", "rs", "xn", "t") as (block, s):
            @block.vector
            def _(dve):
                for t in range(TILES):
                    last = nc.vector.bn_stats(st[:, t], R.h[:, t])
                last.then_inc(s.st, 1)
                dve.wait_ge(s.st, 1)
                for t in range(TILES):
                    last = nc.vector.bn_aggr(mv[:, t], st[:, t])
                last.then_inc(s.mv, 1)
                dve.wait_ge(s.sd, 1)
                nc.vector.reciprocal(rs[:], sd[:]).then_inc(s.rs, 1)
                dve.wait_ge(s.rs, 1)
                for t in range(TILES):
                    nc.vector.tensor_scalar(R.xn[:, t], R.h[:, t], mv[:, t, 0:1], rs[:, t:t + 1],
                                            ALU.subtract, ALU.mult).then_inc(s.xn, 1)
                for q in range(1, 8, 2):
                    dve.wait_ge(s.t, q + 1)
                    nc.vector.tensor_copy(R.xnT[:, q % KC, (q // KC) * 512:(q // KC + 1) * 512], ps[q][0:KP, :])

            @block.scalar
            def _(act):
                act.wait_ge(s.mv, 1)
                nc.scalar.activation(sd[:], mv[:, :, 1], ACT.Sqrt, bias=R.eps[:]).then_inc(s.sd, 1)
                for q in range(0, 8, 2):
                    act.wait_ge(s.t, q + 1)
                    nc.scalar.activation(R.xnT[:, q % KC, (q // KC) * 512:(q // KC + 1) * 512],
                                         ps[q][0:KP, :], ACT.Copy)

            @block.tensor
            def _(pe):
                for g in range(4):
                    pe.wait_ge(s.xn, 4 * g + 4)
                    for c in range(KC):
                        for j in range(4):
                            last = nc.tensor.transpose(ps[g * KC + c][0:KP, j * P:(j + 1) * P],
                                                       R.xn[:, 4 * g + j, c * KP:(c + 1) * KP], R.ident[:])
                        last.then_inc(s.t, 1)



def project_heads(nc, R, tag, wT, bT, outs, wV, bV, V):
    G = len(outs)
    cols = V.shape[2]
    halves = 2 if cols > 512 else 1
    half = cols // halves
    with Mem(nc, tag) as m:
        w = m.sb("w", [KP, KC, G * P])
        wv = m.sb("wv", [KP, KC, cols])
        bt = m.sb("bt", [P, G])
        bv = m.sb("bv", [P, cols])
        ps = [m.ps(f"p{k}", [P, 512]) for k in range(8)]
        with phase(nc, tag, "w", "wv", "z", "mm", "a", "v") as (block, s):
            @block.sync
            def _(sp):
                sp.dma_start(w[:], wT).then_inc(s.w, 16)
                sp.dma_start(wv[:], wV).then_inc(s.wv, 16)
                if bT is not None:
                    sp.dma_start(bt[:], bT).then_inc(s.w, 16)
                    sp.dma_start(bv[:], row(bV)).then_inc(s.wv, 16)

            nT, nV = G * NB, TILES * halves
            total = nT + nV
            have = 16 if bT is None else 32

            @block.tensor
            def _(pe):
                pe.wait_ge(s.w, have)
                for n in range(total):
                    if n == nT:
                        pe.wait_ge(s.wv, have)
                    if n >= 8:
                        pe.wait_ge((s.a, s.v)[n % 2], (n - 8) // 2 + 1)
                    for c in range(KC):
                        if n < nT:
                            g, b = divmod(n, NB)
                            last = nc.tensor.matmul(ps[n % 8][:], w[:, c, g * P:(g + 1) * P],
                                                    R.xnT[:, c, b * BLK:(b + 1) * BLK],
                                                    start=(c == 0), stop=(c == KC - 1))
                        else:
                            t, q = divmod(n - nT, halves)
                            last = nc.tensor.matmul(ps[n % 8][:, 0:half], R.xnT[:, c, t * P:(t + 1) * P],
                                                    wv[:, c, q * half:(q + 1) * half],
                                                    start=(c == 0), stop=(c == KC - 1))
                    last.then_inc(s.mm, 1)

            @block.scalar
            def _(act):
                if bT is not None:
                    act.wait_ge(s.w, have)
                for n in range(0, total, 2):
                    act.wait_ge(s.mm, n + 1)
                    if n < nT:
                        g, b = divmod(n, NB)
                        dst = outs[g][:, b * BLK:(b + 1) * BLK]
                        if bT is None:
                            nc.scalar.activation(dst, ps[n % 8][:], ACT.Copy).then_inc(s.a, 1)
                        else:
                            nc.scalar.activation(dst, ps[n % 8][:], ACT.Identity, bias=bt[:, g:g + 1]).then_inc(s.a, 1)
                    else:
                        t, q = divmod(n - nT, halves)
                        nc.scalar.activation(V[:, t, q * half:(q + 1) * half], ps[n % 8][:, 0:half],
                                             ACT.Copy).then_inc(s.a, 1)

            @block.vector
            def _(dve):
                if bT is not None:
                    dve.wait_ge(s.w, have)
                for n in range(1, total, 2):
                    dve.wait_ge(s.mm, n + 1)
                    if n < nT:
                        g, b = divmod(n, NB)
                        dst = outs[g][:, b * BLK:(b + 1) * BLK]
                        if bT is None:
                            nc.vector.tensor_copy(dst, ps[n % 8][:]).then_inc(s.v, 1)
                        else:
                            nc.vector.tensor_scalar(dst, ps[n % 8][:], bt[:, g:g + 1], None, ALU.add).then_inc(s.v, 1)
                    else:
                        t, q = divmod(n - nT, halves)
                        nc.vector.tensor_copy(V[:, t, q * half:(q + 1) * half], ps[n % 8][:, 0:half]).then_inc(s.v, 1)
                if bT is not None:
                    dve.wait_ge(s.wv, have)
                    dve.wait_ge(s.a, total // 2)
                    dve.wait_ge(s.v, total // 2)
                    nc.vector.tensor_tensor(V[:], V[:], bv[:].unsqueeze(1).broadcast_to([P, TILES, cols]), ALU.add)


def project_out(nc, R, tag, aT, G, wO, bO):
    with Mem(nc, tag) as m:
        w = m.sb("w", [P, G, D])
        bb = m.sb("bb", [P, D])
        ps = [m.ps(f"p{k}", [P, 512]) for k in range(8)]
        with phase(nc, tag, "w", "b", "mm", "hb", "v") as (block, s):
            @block.sync
            def _(sp):
                sp.dma_start(w[:], wO).then_inc(s.w, 16)
                sp.dma_start(bb[:], row(bO)).then_inc(s.b, 16)

            @block.gpsimd
            def _(pool):
                pool.wait_ge(s.b, 16)
                nc.gpsimd.tensor_tensor(R.h[:], R.h[:], bb[:].unsqueeze(1).broadcast_to([P, TILES, D]),
                                        ALU.add).then_inc(s.hb, 1)

            @block.tensor
            def _(pe):
                pe.wait_ge(s.w, 16)
                for t in range(TILES):
                    if t >= 8:
                        pe.wait_ge(s.v, t - 7)
                    for g in range(G):
                        last = nc.tensor.matmul(ps[t % 8][:, 0:D], aT[:, g, t * P:(t + 1) * P], w[:, g],
                                                start=(g == 0), stop=(g == G - 1))
                    last.then_inc(s.mm, 1)

            @block.vector
            def _(dve):
                dve.wait_ge(s.hb, 1)
                for t in range(TILES):
                    dve.wait_ge(s.mm, t + 1)
                    nc.vector.tensor_tensor(R.h[:, t], ps[t % 8][:, 0:D], R.h[:, t], ALU.add).then_inc(s.v, 1)



def attend(nc, R, tag, pairs, krows, scale, V, vw, aT, causal=None, keep=None):
    hpg = P // vw
    with Mem(nc, tag) as m:
        pr = m.sb("pr", [P, 2, 12, SEQ])
        pt = m.sb("pt", [P, 12, SEQ])
        mx = m.sb("mx", [P, 12])
        sm = m.sb("sm", [P, 12])
        rc = m.sb("rc", [P, 12])
        if causal is not None:
            tri = m.sb("tri", [P, SEQ])
            pen = m.sb("pen", [P, 12, SEQ])
        if keep is not None:
            M0, w, half_ones = keep
            dn = m.sb("dn", [P, 12])
            rd = m.sb("rd", [P, 12])
        pS = m.ps("S", [P, 4, 512])
        pT = m.ps("T", [P, 3, 512])
        pX = m.ps("X", [P, 512])
        Sv = pS[:, :, 0:3 * SEQ]
        with phase(nc, tag, "s", "tri", "p", "pe1", "mxd", "ex", "pn", "t", "eA", "eV", "pv", "pv0", "oA", "oV", "v", "z", "g") as (block, s):
            if causal is not None:
                @block.sync
                def _(sp):
                    sp.dma_start(tri[:], causal).then_inc(s.tri, 16)

            @block.tensor
            def _(pe):
                def scores(t):
                    if t >= 1:
                        pe.wait_ge(s.mxd, t)
                    for b in range(2):
                        lo = t * P + b * SEQ
                        for g in range(3):
                            for j in range(4):
                                rows = slice(32 * j, 32 * j + krows)
                                for k, (q, kk) in enumerate(pairs):
                                    last = nc.tensor.matmul(
                                        pS[64 * b:64 * b + 64, j, g * SEQ:(g + 1) * SEQ],
                                        q[rows, g, lo:lo + SEQ], kk[rows, g, lo:lo + SEQ],
                                        start=(k == 0), stop=(k == len(pairs) - 1), skip_group_check=True)
                    last.then_inc(s.s, 1)

                def rest(t):
                    pe.wait_ge(s.pn, t + 1)
                    if t >= 1:
                        pe.wait_ge(s.oA, t)
                        pe.wait_ge(s.oV, t)
                    for sl in range(12):
                        last = nc.tensor.transpose(pT[0:SEQ, sl // 4, (sl % 4) * P:(sl % 4 + 1) * P],
                                                   pr[:, t % 2, sl], R.ident[:])
                    last.then_inc(s.t, 1)
                    pe.wait_ge(s.eA, t + 1)
                    pe.wait_ge(s.eV, t + 1)
                    if keep is None:
                        for b in range(2):
                            if b == 1:
                                pe.wait_ge(s.pv0, t + 1)
                            for sl, h in enumerate(SLOTS):
                                o = (h % hpg) * vw
                                last = nc.tensor.matmul(
                                    pT[o:o + vw, b, (h // hpg) * SEQ:(h // hpg + 1) * SEQ],
                                    V[64 * b:64 * b + 64, t, h * vw:(h + 1) * vw],
                                    pt[64 * b:64 * b + 64, sl], start=True, stop=True)
                            last.then_inc(s.pv0 if b == 0 else s.pv, 1)
                    else:
                        for q in range(2):
                            last = nc.tensor.matmul((pT[:, 2], pX[:])[q][:, 0:6 * SEQ], half_ones[:],
                                                    pr[:, t % 2, 6 * q:6 * q + 6].rearrange("p a b -> p (a b)"), start=True, stop=True)
                        last.then_inc(s.pe1, 1)
                        for k in range(12):
                            for b in range(2):
                                sl = (k + 6 * b) % 12
                                last = nc.tensor.matmul(
                                    pT[64 * b:64 * b + 64, sl // 6, (sl % 6) * SEQ:(sl % 6 + 1) * SEQ],
                                    pt[64 * b:64 * b + 64, sl], pt[64 * b:64 * b + 64, sl], start=True, stop=True)
                        last.then_inc(s.pv0, 1)
                        pe.wait_ge(s.pv0, t + 1)
                        pe.wait_ge(s.g, t + 1)
                        for b in range(2):
                            bank = (pT[:, 2], pX[:])[b]
                            for sl, h in enumerate(SLOTS):
                                last = nc.tensor.matmul(bank[64 * b:64 * b + 64, sl * vw:(sl + 1) * vw],
                                                        pt[64 * b:64 * b + 64, sl],
                                                        V[64 * b:64 * b + 64, t, h * vw:(h + 1) * vw],
                                                        start=True, stop=True)
                        last.then_inc(s.pv, 1)

                scores(0)
                for t in range(TILES):
                    if t + 1 < TILES:
                        scores(t + 1)
                    rest(t)

            @block.vector
            def _(dve):
                own = Own(dve, s.v)
                if causal is not None:
                    dve.wait_ge(s.tri, 16)
                def probs(t):
                    p = pr[:, t % 2]
                    dve.wait_ge(s.s, t + 1)
                    if t >= 2:
                        dve.wait_ge(s.pv, t - 1)
                    if causal is None:
                        own.link(nc.vector.tensor_reduce(mx[:], Sv.rearrange("p j (g k) -> p j g k", g=3), AX.X, ALU.max))
                        nc.vector.tensor_tensor(p.rearrange("p (j g) k -> p j g k", j=4),
                                                Sv.rearrange("p j (g k) -> p j g k", g=3),
                                                mx[:].rearrange("p (j g) -> p j g", j=4).unsqueeze(3).broadcast_to([P, 4, 3, SEQ]),
                                                ALU.subtract).then_inc(s.mxd, 1)
                    else:
                        for j in range(4):
                            last = nc.vector.tensor_tensor(p[:, 3 * j:3 * j + 3], pS[:, j, 0:3 * SEQ].rearrange("p (g k) -> p g k", g=3),
                                                           tri[:].unsqueeze(1).broadcast_to([P, 3, SEQ]), ALU.mult)
                        last.then_inc(s.mxd, 1)
                        dve.wait_ge(s.mxd, t + 1)
                        own.link(nc.vector.tensor_scalar(pen[:], p, 0.0, -1e30, ALU.is_equal, ALU.mult))
                        own.link(nc.vector.tensor_tensor(p, p, pen[:], ALU.add))
                        own.link(nc.vector.tensor_reduce(mx[:], p, AX.X, ALU.max))
                        nc.vector.tensor_tensor(p, p, mx[:].unsqueeze(2).broadcast_to([P, 12, SEQ]), ALU.subtract).then_inc(s.p, 1)
                def norm(t):
                    p = pr[:, t % 2]
                    dve.wait_ge(s.ex, t + 1)
                    own.link(nc.vector.tensor_reduce(sm[:], p, AX.X, ALU.add))
                    own.link(nc.vector.reciprocal(rc[:], sm[:]))
                    nc.vector.tensor_tensor(p, p, rc[:].unsqueeze(2).broadcast_to([P, 12, SEQ]), ALU.mult).then_inc(s.pn, 1)
                def evac(t):
                    dve.wait_ge(s.t, t + 1)
                    for b in range(2):
                        last = nc.vector.tensor_copy(
                            pt[64 * b:64 * b + 64, 0:4],
                            pT[0:SEQ, 0].rearrange("p (s b n) -> p s b n", b=2, n=SEQ)[:, :, b])
                    last.then_inc(s.eV, 1)
                def outs(t):
                    if keep is None:
                        dve.wait_ge(s.pv, t + 1)
                        nc.vector.tensor_copy(aT[:, :, t * P:t * P + SEQ],
                                              pT[:, 0, 0:aT.shape[1] * SEQ].rearrange("p (g n) -> p g n", n=SEQ)).then_inc(s.oV, 1)
                    else:
                        dve.wait_ge(s.pe1, t + 1)
                        own.mark(nc.vector.tensor_reduce(dn[:, 0:6], pT[:, 2, 0:6 * SEQ].rearrange("p (s k) -> p s k", k=SEQ), AX.X, ALU.max))
                        nc.vector.tensor_reduce(dn[:, 6:12], pX[:, 0:6 * SEQ].rearrange("p (s k) -> p s k", k=SEQ), AX.X, ALU.max).then_inc(s.g, 1)
                        dve.wait_ge(s.g, t + 1)
                        own.settle()
                        own.link(nc.vector.reciprocal(rd[:], dn[:]))
                        dve.wait_ge(s.pv0, t + 1)
                        nc.vector.tensor_tensor(M0[:, t].rearrange("p (q s) k -> p q s k", q=2),
                                                pT[:, 0:2, 0:6 * SEQ].rearrange("p q (s k) -> p q s k", k=SEQ),
                                                rd[:].rearrange("p (q s) -> p q s", q=2).unsqueeze(3).broadcast_to([P, 2, 6, SEQ]),
                                                ALU.mult).then_inc(s.oV, 1)
                probs(0)
                for t in range(TILES):
                    norm(t)
                    if t + 1 < TILES:
                        probs(t + 1)
                    evac(t)
                    outs(t)

            @block.scalar
            def _(act):
                def exps(t):
                    act.wait_ge(s.mxd if causal is None else s.p, t + 1)
                    nc.scalar.activation(pr[:, t % 2], pr[:, t % 2], ACT.Exp, scale=scale).then_inc(s.ex, 1)
                exps(0)
                for t in range(TILES):
                    act.wait_ge(s.t, t + 1)
                    for b in range(2):
                        last = nc.scalar.activation(
                            pt[64 * b:64 * b + 64, 4:12].rearrange("p (q s) n -> p q s n", q=2),
                            pT[0:SEQ, 1:3].rearrange("p q (s b n) -> p q s b n", b=2, n=SEQ)[:, :, :, b], ACT.Copy)
                    last.then_inc(s.eA, 1)
                    if t + 1 < TILES:
                        exps(t + 1)
                    act.wait_ge(s.pv, t + 1)
                    if keep is None:
                        nc.scalar.activation(aT[:, :, t * P + SEQ:(t + 1) * P],
                                             pT[:, 1, 0:aT.shape[1] * SEQ].rearrange("p (g n) -> p g n", n=SEQ),
                                             ACT.Copy).then_inc(s.oA, 1)
                    else:
                        nc.scalar.activation(w[0:SEQ, t], pT[0:SEQ, 2, 0:12 * vw], ACT.Copy)
                        nc.scalar.activation(w[SEQ:P, t], pX[SEQ:P, 0:12 * vw], ACT.Copy).then_inc(s.oA, 1)



def chunked(wT):
    return wT.reshape(KC, KP, -1).transpose(1, 0, 2)


def head_pad(w, hd, width=32):
    out = np.zeros(w.shape[:-1] + (HEADS, width), w.dtype)
    out[..., :hd] = w.reshape(w.shape[:-1] + (HEADS, hd))
    return out.reshape(w.shape[:-1] + (HEADS * width,))


def grouped(v):
    return v.reshape(-1, P).T


def layout(a):
    z = {}
    xp = np.zeros((IMAGES, SIDE + 2, SIDE + 2, CH), a["x"].dtype)
    xp[:, 1:-1, 1:-1] = a["x"]
    py = np.arange(GRID) * PATCH
    rr = np.array([r for r, _ in HALO]) + 1
    cc = np.array([c for _, c in HALO]) + 1
    rows = py[:, None, None] + rr[None, None, :]
    cols = py[None, :, None] + cc[None, None, :]
    pix = xp[:, rows, cols]
    pix = pix.reshape(TILES, P, HK, HP).transpose(0, 3, 2, 1)
    z["x"] = pix
    at = {rc: i for i, rc in enumerate(HALO)}
    W = a["L0_tok_W"].reshape(PATCH, PATCH, len(SHIFTS), CH, D)
    ls = a["L0_tok_ln_scale"].reshape(PATCH, PATCH, len(SHIFTS), CH)
    wsh = np.zeros((len(HALO), CH, len(SHIFTS), D), W.dtype)
    lsh = np.zeros((len(HALO), CH, len(SHIFTS)), ls.dtype)
    mult = np.zeros((len(HALO), CH), np.float32)
    for j, (dr, dc) in enumerate(SHIFTS):
        where = np.array([at[(r + dr, c + dc)] for r in range(PATCH) for c in range(PATCH)])
        wsh[where, :, j] = W[:, :, j].reshape(PATCH * PATCH, CH, D)
        lsh[where, :, j] = ls[:, :, j].reshape(PATCH * PATCH, CH)
        mult[where] += 1.0
    z["tok_w"] = wsh.reshape(HK, HP, len(SHIFTS), D).transpose(1, 0, 2, 3)
    z["tok_ln"] = lsh.reshape(HK, HP, len(SHIFTS)).transpose(1, 0, 2)
    z["tok_mult"] = mult.reshape(HK, HP).T
    z["tok_b"] = a["L0_tok_b"]
    hd = D // HEADS
    wq, wk, wv = np.split(a["L0_attn_qkv_w"].T, 3, axis=1)
    bq, bk, bv = np.split(a["L0_attn_qkv_b"], 3)
    z["a0_wT"] = chunked(np.concatenate([head_pad(wq, hd), head_pad(wk, hd)], 1))
    z["a0_bT"] = grouped(np.concatenate([head_pad(bq, hd), head_pad(bk, hd)]))
    z["a0_wV"] = chunked(head_pad(wv, hd))
    z["a0_bV"] = head_pad(bv, hd)
    z["a0_wO"] = head_pad(a["L0_attn_proj_w"], hd).T.reshape(3, P, D).transpose(1, 0, 2)
    z["a0_bO"] = a["L0_attn_proj_b"]
    more_layout(a, z)
    return {k: np.ascontiguousarray(v) for k, v in z.items()}



def experts(nc, R, tag, E, F, up, down, act_fn, glu, coef, acc, bias=None):
    FC = F // P
    W2 = 2 if glu else 1
    RING = 2 if glu else 4
    with Mem(nc, tag) as m:
        wu = m.sb("wu", [KP, 2, KC, W2 * F])
        wd = m.sb("wd", [P, 2, FC, D])
        bi = m.sb("bi", [P, 2, FC]) if bias is not None else None
        hT = m.sb("hT", [P, 2, FC, BLK])
        sg = m.sb("sg", [P, 2, BLK]) if glu else None
        up_ps = [m.ps(f"u{k}", [P, 512]) for k in range(4)]
        dn_ps = [m.ps(f"d{k}", [P, 512]) for k in range(4)]
        pairs = (E + 1) // 2
        per_e = NB * FC

        def each(eng):
            if E == 1:
                yield 0, 0
            else:
                with eng.Fori(0, pairs) as i:
                    for u in range(2):
                        yield i * 2 + u, u

        with phase(nc, tag, "w0", "w1", "up", "hid", "gate", "down", "acc") as (block, s):
            @block.sync
            def _(sp):
                for e, u in each(sp):
                    sp.wait_ge(s.acc, e * TILES + TILES if E > 1 else 0)
                    sp.dma_start(wu[:, u], up[e]).then_inc((s.w0, s.w1)[u], 16)
                    if bias is not None:
                        sp.dma_start(bi[:, u], bias[e]).then_inc((s.w0, s.w1)[u], 16)
                    sp.dma_start(wd[:, u], down[e]).then_inc((s.w0, s.w1)[u], 16)

            loads = 3 if bias is not None else 2

            def weights_in(eng, e, u):
                eng.wait_ge((s.w0, s.w1)[u], (e - u) * (8 * loads) + 16 * loads)

            @block.tensor
            def _(pe):
                nc.tensor.sem_inc(s.down, 8)

                def go_up(e, u, b):
                    for f in range(FC):
                        n = e * per_e + (b * FC + f)
                        pe.wait_ge(s.hid, n + 1)
                        k = (b * FC + f) % RING
                        for q in range(W2):
                            for c in range(KC):
                                last = nc.tensor.matmul(up_ps[W2 * k + q][:], wu[:, u, c, q * F + f * P:q * F + (f + 1) * P],
                                                        R.xnT[:, c, b * BLK:(b + 1) * BLK],
                                                        start=(c == 0), stop=(c == KC - 1))
                        last.then_inc(s.up, 1)

                def go_down(e, u, b):
                    for j in range(4):
                        d = e * TILES + (b * 4 + j)
                        pe.wait_ge(s.acc, d + 29)
                        for f in range(FC):
                            if j == 0:
                                pe.wait_ge(s.hid, e * per_e + (b * FC + f + 1 + RING))
                            last = nc.tensor.matmul(dn_ps[j][:, 0:D], hT[:, b % 2, f, j * P:(j + 1) * P], wd[:, u, f],
                                                    start=(f == 0), stop=(f == FC - 1))
                        last.then_inc(s.down, 1)

                for e, u in each(pe):
                    weights_in(pe, e, u)
                    go_up(e, u, 0)
                    for b in range(1, NB):
                        go_up(e, u, b)
                        go_down(e, u, b - 1)
                    go_down(e, u, NB - 1)

            @block.scalar
            def _(act):
                if not glu:
                    nc.scalar.sem_inc(s.hid, RING)
                for e, u in each(act):
                    if bias is not None:
                        weights_in(act, e, u)
                    for b in range(NB):
                        for f in range(FC):
                            n = e * per_e + (b * FC + f)
                            act.wait_ge(s.up, n + 1)
                            k = (b * FC + f) % RING
                            if glu:
                                act.wait_ge(s.hid, n + 1)
                                nc.scalar.activation(sg[:, k], up_ps[2 * k][:], act_fn).then_inc(s.gate, 1)
                            else:
                                if f == 0:
                                    act.wait_ge(s.down, e * TILES + (4 * b + 4))
                                nc.scalar.activation(hT[:, b % 2, f], up_ps[k][:], act_fn,
                                                     bias=bi[:, u, f:f + 1]).then_inc(s.hid, 1)

            @block.vector
            def _(dve):
                nc.vector.sem_inc(s.acc, 32)
                if glu:
                    nc.vector.sem_inc(s.hid, RING)

                def gated(e, u, b):
                    for f in range(FC):
                        n = e * per_e + (b * FC + f)
                        k = (b * FC + f) % RING
                        dve.wait_ge(s.gate, n + 1)
                        if f == 0:
                            dve.wait_ge(s.down, e * TILES + (4 * b + 4))
                        nc.vector.tensor_tensor(hT[:, b % 2, f], up_ps[2 * k + 1][:], sg[:, k], ALU.mult).then_inc(s.hid, 1)

                def gather(e, u, b):
                    for j in range(4):
                        d = e * TILES + (b * 4 + j)
                        dve.wait_ge(s.down, d + 9)
                        dve.wait_ge(s.acc, d + 17)
                        t = b * 4 + j
                        if coef is None:
                            nc.vector.tensor_tensor(acc[:, t], dn_ps[j][:, 0:D], acc[:, t], ALU.add).then_inc(s.acc, 1)
                        else:
                            nc.vector.scalar_tensor_tensor(acc[:, t], dn_ps[j][:, 0:D], coef(t, e), acc[:, t],
                                                           ALU.mult, ALU.add).then_inc(s.acc, 1)

                for e, u in each(dve):
                    if glu:
                        gated(e, u, 0)
                        for b in range(1, NB):
                            gated(e, u, b)
                            gather(e, u, b - 1)
                        gather(e, u, NB - 1)
                    else:
                        for b in range(NB):
                            gather(e, u, b)


def logits(nc, pe, R, ps, w, n):
    for t in range(TILES):
        for c in range(KC):
            last = nc.tensor.matmul(ps[:, t * n:(t + 1) * n], R.xnT[:, c, t * P:(t + 1) * P], w[:, c],
                                    start=(c == 0), stop=(c == KC - 1), skip_group_check=True)
    return last


def ffn0(nc, R, I):
    E = 8
    with Mem(nc, "f0") as m:
        coef = m.sb("coef", [P, TILES, E])
        with Mem(nc, "f0r") as r:
            wr = r.sb("wr", [KP, KC, E])
            bo = r.sb("bo", [E, D])
            io = r.sb("io", [P, E])
            lg = r.sb("lgs", [P, TILES, E])
            top = r.sb("top", [P, TILES, 8])
            idx = r.sb("idx", [P, TILES, 8], U32)
            idf = r.sb("idf", [P, TILES, 8])
            g = r.sb("g", [P, 4, TILES])
            c2 = r.sb("c2", [P, TILES, E])
            cT = r.sb("cT", [E, TILES, P])
            ps = r.ps("lg", [P, 512])
            pt = r.ps("ct", [P, 4, 512])
            pb = [r.ps(f"b{k}", [P, 512]) for k in range(3)]
            with phase(nc, "f0r", "w", "io", "lg", "v", "ex", "co", "t", "ct", "mm", "b") as (block, s):
                @block.sync
                def _(sp):
                    sp.dma_start(wr[:], I["f0_wr"]).then_inc(s.w, 16)
                    sp.dma_start(bo[:], I["f0_bo"]).then_inc(s.w, 16)

                @block.gpsimd
                def _(pool):
                    nc.gpsimd.iota(io[:], [[1, E]], base=0, channel_multiplier=0,
                                   allow_small_or_imprecise_dtypes=True).then_inc(s.io, 1)

                @block.tensor
                def _(pe):
                    pe.wait_ge(s.w, 32)
                    logits(nc, pe, R, ps, wr, E).then_inc(s.lg, 1)
                    pe.wait_ge(s.co, 1)
                    for t in range(TILES):
                        last = nc.tensor.transpose(pt[0:E, t // 4, (t % 4) * P:(t % 4 + 1) * P], coef[:, t], R.ident[:])
                    last.then_inc(s.t, 1)
                    pe.wait_ge(s.ct, 1)
                    for t in range(TILES):
                        if t >= 3:
                            pe.wait_ge(s.b, t - 2)
                        nc.tensor.matmul(pb[t % 3][:, 0:D], cT[:, t], bo[:], start=True, stop=True).then_inc(s.mm, 1)

                @block.scalar
                def _(act):
                    act.wait_ge(s.v, 1 + TILES + 2)
                    nc.scalar.activation(g[:, 1], g[:, 0], ACT.Exp).then_inc(s.ex, 1)

                @block.vector
                def _(dve):
                    own = Own(dve, s.v)
                    dve.wait_ge(s.lg, 1)
                    own.link(nc.vector.tensor_copy(lg[:], ps[:, 0:TILES * E].rearrange("p (t e) -> p t e", e=E)))
                    for t in range(TILES):
                        own.mark(nc.vector.max(top[:, t], lg[:, t]))
                    own.settle()
                    own.mark(nc.vector.tensor_tensor(g[:, 0], top[:, :, 1], top[:, :, 0], ALU.subtract))
                    for t in range(TILES):
                        last = nc.vector.max_index(idx[:, t], top[:, t], lg[:, t])
                    own.link(last)
                    own.link(nc.vector.tensor_copy(idf[:], idx[:]))
                    dve.wait_ge(s.ex, 1)
                    own.link(nc.vector.tensor_scalar(g[:, 0], g[:, 1], 1.0, None, ALU.add))
                    own.link(nc.vector.reciprocal(g[:, 2], g[:, 0]))
                    own.link(nc.vector.tensor_tensor(g[:, 3], g[:, 1], g[:, 2], ALU.mult))
                    dve.wait_ge(s.io, 1)
                    iob = io[:].unsqueeze(1).broadcast_to([P, TILES, E])
                    for k, dst in ((0, coef), (1, c2)):
                        own.link(nc.vector.tensor_tensor(dst[:], iob, idf[:, :, k:k + 1].broadcast_to([P, TILES, E]), ALU.is_equal))
                        own.link(nc.vector.tensor_tensor(dst[:], dst[:], g[:, 2 + k].unsqueeze(2).broadcast_to([P, TILES, E]), ALU.mult))
                    nc.vector.tensor_tensor(coef[:], coef[:], c2[:], ALU.add).then_inc(s.co, 1)
                    dve.wait_ge(s.t, 1)
                    nc.vector.tensor_copy(cT[:].rearrange("e (a b) p -> e a (b p)", a=4), pt[0:E]).then_inc(s.ct, 1)
                    for t in range(TILES):
                        dve.wait_ge(s.mm, t + 1)
                        nc.vector.tensor_tensor(R.h[:, t], pb[t % 3][:, 0:D], R.h[:, t], ALU.add).then_inc(s.b, 1)
        experts(nc, R, "f0e", E, 768, I["f0_up"], I["f0_down"], ACT.Gelu, False,
                lambda t, e: coef[:, t, bass.ds(e, 1)], R.h, bias=I["f0_bi"])



def attention1(nc, R, I):
    with Mem(nc, "a1") as m:
        V = m.sb("V", [P, TILES, 12 * 64])
        Q = m.sb("Q", [P, 6, TOK])
        with Mem(nc, "a1k") as mk:
            K = mk.sb("K", [P, 6, TOK])
            project_heads(nc, R, "a1p", I["a1_wT"], I["a1_bT"],
                          [Q[:, g] for g in range(6)] + [K[:, g] for g in range(6)], I["a1_wV"], I["a1_bV"], V[:])
            rotate(nc, R, I, Q, K)
            attend(nc, R, "a1a", [(Q[:, 0:3], K[:, 0:3]), (Q[:, 3:6], K[:, 3:6])], 32, 0.125, V[:], 64, Q[:],
                   causal=I["a1_tri"])
        project_out(nc, R, "a1o", Q, 6, I["a1_wO"], I["a1_bO"])


def rotate(nc, R, I, Q, K):
    with Mem(nc, "rot") as m:
        cs = m.sb("cs", [P, 2, SEQ])
        a = m.sb("a", [P, 2, 2, BLK])
        b = m.sb("b", [P, 2, 2, BLK])
        with phase(nc, "rot", "w", "a", "b", "v") as (block, s):
            work = [(T, g, k) for T in (Q, K) for g in range(3) for k in range(NB)]

            def view(ap):
                return ap.rearrange("p (i t) -> p i t", t=SEQ)

            def table(k):
                return cs[:, k].unsqueeze(1).broadcast_to([P, BLK // SEQ, SEQ])

            @block.sync
            def _(sp):
                sp.dma_start(cs[:], I["a1_cs"]).then_inc(s.w, 16)

            @block.gpsimd
            def _(pool):
                pool.wait_ge(s.w, 16)
                for n, (T, g, k) in enumerate(work):
                    if n >= 2:
                        pool.wait_ge(s.v, 2 * (n - 1))
                    for part in range(2):
                        src = T[:, 3 * part + g, k * BLK:(k + 1) * BLK]
                        nc.gpsimd.tensor_tensor(view(a[:, n % 2, part]), view(src), table(0), ALU.mult).then_inc(s.a, 1)

            @block.vector
            def _(dve):
                dve.wait_ge(s.w, 16)
                for n, (T, g, k) in enumerate(work):
                    for part in range(2):
                        src = T[:, 3 * part + g, k * BLK:(k + 1) * BLK]
                        last = nc.vector.tensor_tensor(view(b[:, n % 2, part]), view(src), table(1), ALU.mult)
                    last.then_inc(s.b, 1)
                    dve.wait_ge(s.b, n + 1)
                    dve.wait_ge(s.a, 2 * (n + 1))
                    nc.vector.tensor_tensor(T[:, g, k * BLK:(k + 1) * BLK], a[:, n % 2, 0], b[:, n % 2, 1], ALU.subtract).then_inc(s.v, 1)
                    nc.vector.tensor_tensor(T[:, 3 + g, k * BLK:(k + 1) * BLK], a[:, n % 2, 1], b[:, n % 2, 0], ALU.add).then_inc(s.v, 1)


def ffn1(nc, R, I):
    E, CAP = 16, TOK // 16 * 2
    with Mem(nc, "f1") as m:
        coef = m.sb("coef", [P, TILES, E])
        with Mem(nc, "f1r") as r:
            wr = r.sb("wr", [KP, KC, E])
            sc = r.sb("sc", [E, TOK])
            wk = r.sb("wk", [E, TOK])
            top = r.sb("top", [E, 8])
            ps = [r.ps(f"lg{k}", [P, 512]) for k in range(4)]
            pc = r.ps("pc", [P, 512])
            with phase(nc, "f1r", "w", "lg", "sg", "v", "m", "t") as (block, s):
                @block.sync
                def _(sp):
                    sp.dma_start(wr[:], I["f1_gate"]).then_inc(s.w, 16)

                @block.tensor
                def _(pe):
                    pe.wait_ge(s.w, 16)
                    for b in range(NB):
                        for c in range(KC):
                            last = nc.tensor.matmul(ps[b][0:E, :], wr[:, c], R.xnT[:, c, b * BLK:(b + 1) * BLK],
                                                    start=(c == 0), stop=(c == KC - 1))
                        last.then_inc(s.lg, 1)
                    pe.wait_ge(s.m, 1)
                    for t in range(TILES):
                        last = nc.tensor.transpose(pc[:, t * E:(t + 1) * E], sc[:, t * P:(t + 1) * P], R.ident[0:E, 0:E])
                    last.then_inc(s.t, 1)

                @block.scalar
                def _(act):
                    for b in range(NB):
                        act.wait_ge(s.lg, b + 1)
                        nc.scalar.activation(sc[:, b * BLK:(b + 1) * BLK], ps[b][0:E, :], ACT.Sigmoid).then_inc(s.sg, 1)

                @block.vector
                def _(dve):
                    dve.wait_ge(s.sg, NB)
                    own = Own(dve, s.v)
                    own.link(nc.vector.tensor_copy(wk[:], sc[:]))
                    for _ in range(CAP // 8):
                        own.link(nc.vector.max(top[:], wk[:]))
                        own.link(nc.vector.match_replace(wk[:], top[:], wk[:], -1.0))
                    own.link(nc.vector.tensor_scalar(wk[:], wk[:], 0.0, None, ALU.is_lt))
                    nc.vector.tensor_tensor(sc[:], sc[:], wk[:], ALU.mult).then_inc(s.m, 1)
                    dve.wait_ge(s.t, 1)
                    nc.vector.tensor_copy(coef[:].rearrange("p t e -> p (t e)"), pc[:, 0:TILES * E])
        experts(nc, R, "f1s", 1, 384, I["f1_sup"], I["f1_sdown"], ACT.Silu, True, None, R.h)
        experts(nc, R, "f1e", E, 768, I["f1_up"], I["f1_down"], ACT.Silu, True,
                lambda t, e: coef[:, t, bass.ds(e, 1)], R.h)



def attention2(nc, R, I):
    with Mem(nc, "a2") as m:
        M0 = m.sb("M0", [P, TILES, 12, SEQ])
        w = m.sb("w", [P, TILES, 12 * 32])
        with Mem(nc, "a2q") as mq:
            qk = mq.sb("qk", [P, 6, TOK])
            V = mq.sb("V", [P, TILES, 12 * 32])
            half = mq.sb("half", [P, P])
            project_heads(nc, R, "a2p", I["a2_wT"], None, [qk[:, g] for g in range(6)], I["a2_wV"], None, V[:])
            with phase(nc, "half", "v") as (block, s):
                @block.vector
                def _(dve):
                    nc.vector.memset(half[:], 0.0).then_inc(s.v, 1)
                    dve.wait_ge(s.v, 1)
                    for b in range(2):
                        nc.vector.memset(half[64 * b:64 * b + 64, 64 * b:64 * b + 64], 1.0)
            attend(nc, R, "a2a", [(qk[:, 0:3], qk[:, 3:6])], D // HEADS, (D // HEADS) ** -0.5, V[:], 32, None,
                   keep=(M0, w, half))
        aT = m.sb("aT", [P, 3, TOK])
        newton(nc, R, M0, w, aT)
        project_out(nc, R, "a2o", aT, 3, I["a2_wO"], I["a2_bO"])


def newton(nc, R, M0, w, aT):
    N_ITER = 6
    with Mem(nc, "nw") as m:
        i15 = m.sb("i15", [P, SEQ])
        T = [m.sb(f"T{u}", [P, 12, SEQ]) for u in range(2)]
        Q = [m.sb(f"Q{u}", [P, 12, SEQ]) for u in range(2)]
        p2 = [m.ps(f"p2{u}", [P, 2, 512]) for u in range(2)]
        pz = [m.ps(f"pz{u}", [P, 2, 512]) for u in range(2)]
        steps = [(tp, k, u) for tp in range(0, TILES, 2) for k in range(N_ITER) for u in range(2)]

        def view(ps):
            return ps[:, :, 0:6 * SEQ].rearrange("p q (s k) -> p q s k", k=SEQ)

        def halves(ap):
            return ap.rearrange("p (q s) k -> p q s k", q=2)

        with phase(nc, "nw", "i", "m2", "q", "T", "y", "z", "m", "o0", "o1", "oA", "oV") as (block, s):
            @block.gpsimd
            def _(pool):
                nc.gpsimd.tensor_scalar(i15[0:64, :], R.ident[0:64, 0:64], 15.0, None, ALU.mult).then_inc(s.i, 1)
                nc.gpsimd.tensor_scalar(i15[64:P, :], R.ident[64:P, 64:P], 15.0, None, ALU.mult).then_inc(s.i, 1)
                pool.wait_ge(s.i, 2)
                n_i = 2
                for n, (tp, k, u) in enumerate(steps):
                    if k > 0:
                        pool.wait_ge(s.m, n - 1)
                    if n >= 2:
                        pool.wait_ge(s.z, n - 1)
                    n_i += 1
                    nc.gpsimd.tensor_scalar(T[u][:], M0[:, tp + u], 7.0, None, ALU.mult).then_inc(s.i, 1)
                    pool.wait_ge(s.i, n_i)
                    nc.gpsimd.tensor_tensor(T[u][:], T[u][:], i15[:].unsqueeze(1).broadcast_to([P, 12, SEQ]),
                                            ALU.subtract).then_inc(s.T, 1)

            def product(ps, A, B):
                for k in range(12):
                    for b in range(2):
                        sl = (k + 6 * b) % 12
                        rows = slice(64 * b, 64 * b + 64)
                        last = nc.tensor.matmul(ps[rows, sl // 6, (sl % 6) * SEQ:(sl % 6 + 1) * SEQ],
                                                A[rows, sl], B[rows, sl], start=True, stop=True)
                return last

            @block.tensor
            def _(pe):
                def square(n):
                    tp, k, u = steps[n]
                    if k > 0:
                        pe.wait_ge(s.m, n - 1)
                    elif n >= 2:
                        pe.wait_ge(s.oA if u else s.oV, tp // 2)
                    product(p2[u], M0[:, tp + u], M0[:, tp + u]).then_inc(s.m2, 1)

                def second(n):
                    tp, k, u = steps[n]
                    pe.wait_ge(s.y, n + 1)
                    product(pz[u], Q[u], T[u]).then_inc(s.z, 1)

                def out(n):
                    tp, k, u = steps[n]
                    pe.wait_ge(s.m, n + 1)
                    for b in range(2):
                        rows = slice(64 * b, 64 * b + 64)
                        if b == 1:
                            pe.wait_ge(s.o0, 2 * (tp // 2) + u + 1)
                        for sl, h in enumerate(SLOTS):
                            o = 32 * (h % 4)
                            last = nc.tensor.matmul(p2[u][o:o + 32, b, (h // 4) * SEQ:(h // 4 + 1) * SEQ],
                                                    w[rows, tp + u, sl * 32:(sl + 1) * 32], M0[rows, tp + u, sl],
                                                    start=True, stop=True)
                        last.then_inc(s.o0 if b == 0 else s.o1, 1)

                for n in range(0, len(steps), 2):
                    square(n)
                    square(n + 1)
                    second(n)
                    second(n + 1)
                    if steps[n][1] == N_ITER - 1:
                        out(n)
                        out(n + 1)

            @block.scalar
            def _(act):
                for n, (tp, k, u) in enumerate(steps):
                    act.wait_ge(s.m2, n + 1)
                    if n >= 2:
                        act.wait_ge(s.z, n - 1)
                    nc.scalar.activation(halves(Q[u][:]), view(p2[u]), ACT.Copy, scale=0.25).then_inc(s.q, 1)
                    if k == N_ITER - 1 and u == 1:
                        act.wait_ge(s.o1, tp + 2)
                        nc.scalar.activation(aT[:, :, (tp + 1) * P:(tp + 2) * P].rearrange("p g (b n) -> p b g n", b=2),
                                             p2[1][:, :, 0:3 * SEQ].rearrange("p b (g n) -> p b g n", n=SEQ),
                                             ACT.Copy).then_inc(s.oA, 1)

            @block.vector
            def _(dve):
                def y(n):
                    tp, k, u = steps[n]
                    dve.wait_ge(s.q, n + 1)
                    dve.wait_ge(s.T, n + 1)
                    nc.vector.scalar_tensor_tensor(T[u][:], Q[u][:], -4.0, T[u][:], ALU.mult, ALU.add).then_inc(s.y, 1)

                def step(n):
                    tp, k, u = steps[n]
                    dve.wait_ge(s.z, n + 1)
                    dve.wait_ge(s.T, n + 1)
                    nc.vector.scalar_tensor_tensor(M0[:, tp + u].rearrange("p s k -> p (s k)").rearrange("p (q r) -> p q r", q=2),
                                                   M0[:, tp + u].rearrange("p s k -> p (s k)").rearrange("p (q r) -> p q r", q=2), 3.25,
                                                   pz[u][:, :, 0:6 * SEQ], ALU.mult, ALU.add).then_inc(s.m, 1)

                for n in range(0, len(steps), 2):
                    y(n)
                    y(n + 1)
                    step(n)
                    step(n + 1)
                    tp, k, _ = steps[n]
                    if k == N_ITER - 1:
                        dve.wait_ge(s.o1, tp + 1)
                        nc.vector.tensor_copy(aT[:, :, tp * P:(tp + 1) * P].rearrange("p g (b n) -> p b g n", b=2),
                                              p2[0][:, :, 0:3 * SEQ].rearrange("p b (g n) -> p b g n", n=SEQ)).then_inc(s.oV, 1)



CLS = 6
CLS_PAIRS = [(0, 3), (0, 4), (1, 3), (1, 4), (2, 3), (2, 4)]
USERS = [[i for i in range(CLS) if a in CLS_PAIRS[i]] for a in range(5)]


def ffn2(nc, R, I):
    with Mem(nc, "f2") as m:
        patch = m.sb("ptk", [P, 1])
        pb2 = m.sb("pb2", [P, D])
        with phase(nc, "f2b", "w", "v") as (block, s):
            @block.sync
            def _(sp):
                sp.dma_start(patch[:], I["f2_patch"]).then_inc(s.w, 16)
                sp.dma_start(pb2[:], row(I["f2_b2"])).then_inc(s.w, 16)

            @block.vector
            def _(dve):
                dve.wait_ge(s.w, 32)
                nc.vector.tensor_scalar(pb2[:], pb2[:], patch[:, 0:1], None, ALU.mult).then_inc(s.v, 1)
                dve.wait_ge(s.v, 1)
                nc.vector.tensor_tensor(R.h[:], R.h[:], pb2[:].unsqueeze(1).broadcast_to([P, TILES, D]), ALU.add)
        experts(nc, R, "f2p", 1, 768, I["f2_up"], I["f2_down"], ACT.Gelu, False,
                lambda t, e: patch[:, 0:1], R.h, bias=I["f2_bi"])
        class_tokens(nc, R, I)


def class_tokens(nc, R, I):
    FC = 6
    with Mem(nc, "ct") as m:
        w1 = m.sb("w1", [KP, 5, KC, 768])
        w2 = m.sb("w2", [P, 5, FC, D])
        b1 = m.sb("b1", [P, 5, FC])
        b2 = m.sb("b2", [IMAGES, CLS, 2, D])
        gw = m.sb("gw", [KP, KC, CLS, 2])
        hc = [m.sb(f"hc{a}", [P, FC, len(USERS[a]) * IMAGES]) for a in range(5)]
        lg = m.sb("lg", [IMAGES, CLS, 2])
        gt = m.sb("gt", [IMAGES, CLS, 2])
        mk = m.sb("mk", [IMAGES, CLS, 2])
        r1 = m.sb("r1", [IMAGES, CLS])
        r2 = m.sb("r2", [IMAGES, CLS])
        tmp = m.sb("tmp", [IMAGES, CLS, 2, D])
        co = m.sb("co", [IMAGES, CLS, D])
        dl = m.sb("dl", [P, TILES, D])
        back = nc.dram_tensor("class_out", [IMAGES, CLS, D], F32).ap()
        up_ps = [m.ps(f"u{k}", [P, 512]) for k in range(4)]
        dn_ps = [m.ps(f"d{k}", [P, 512]) for k in range(3)]
        pg = m.ps("g", [P, 512])
        with phase(nc, "ct", "wg", "w1", "w2", "g", "up", "hc", "dn", "v", "ex", "tm", "co", "dz", "st", "ld") as (block, s):
            @block.sync
            def _(sp):
                sp.dma_start(gw[:], I["f2_gw"]).then_inc(s.wg, 16)
                sp.dma_start(b1[:], I["f2_a1b"]).then_inc(s.w1, 16)
                sp.dma_start(w1[:], I["f2_a1"]).then_inc(s.w1, 16)
                sp.dma_start(b2[:], I["f2_a2b"].unsqueeze(0).broadcast_to([IMAGES, CLS, 2, D])).then_inc(s.w2, 16)
                sp.dma_start(w2[:], I["f2_a2"]).then_inc(s.w2, 16)
                sp.wait_ge(s.co, CLS)
                sp.dma_start(back, co[:]).then_inc(s.st, 16)
                sp.wait_ge(s.st, 16)
                sp.wait_ge(s.dz, 1)
                for b in range(2):
                    sp.dma_start(dl[64 * b:64 * b + CLS],
                                 back.rearrange("(t b) i d -> b i t d", b=2)[b]).then_inc(s.ld, 16)

            @block.gpsimd
            def _(pool):
                nc.gpsimd.memset(dl[:], 0.0).then_inc(s.dz, 1)

            def tokens(c, classes):
                step = classes[1] - classes[0]
                v = R.xnT[:, c].rearrange("p (b s) -> p s b", s=SEQ)
                return v[:, classes[0]:classes[-1] + 1:step]

            @block.tensor
            def _(pe):
                pe.wait_ge(s.wg, 16)
                for i in range(CLS):
                    for c in range(KC):
                        last = nc.tensor.matmul(pg[0:IMAGES, 2 * i:2 * i + 2],
                                                R.xnT[:, c].rearrange("p (b s) -> p s b", s=SEQ)[:, i],
                                                gw[:, c, i], start=(c == 0), stop=(c == KC - 1), skip_group_check=True)
                last.then_inc(s.g, 1)
                pe.wait_ge(s.w1, 32)
                n = 0
                for a in range(5):
                    for f in range(FC):
                        if n >= 4:
                            pe.wait_ge(s.hc, n - 3)
                        for c in range(KC):
                            last = nc.tensor.matmul(
                                up_ps[n % 4][:, 0:len(USERS[a]) * IMAGES].rearrange("p (s b) -> p s b", b=IMAGES),
                                w1[:, a, c, f * P:(f + 1) * P], tokens(c, USERS[a]), start=(c == 0), stop=(c == KC - 1))
                        last.then_inc(s.up, 1)
                        n += 1
                pe.wait_ge(s.hc, n)
                pe.wait_ge(s.w2, 32)
                for i in range(CLS):
                    if i >= 3:
                        pe.wait_ge(s.tm, i - 2)
                    a0, a1 = CLS_PAIRS[i]
                    for k, (a, c) in enumerate(((a0, a1), (a1, a0))):
                        at = USERS[a].index(i) * IMAGES
                        for f in range(FC):
                            last = nc.tensor.matmul(dn_ps[i % 3][0:IMAGES, k * D:(k + 1) * D], hc[a][:, f, at:at + IMAGES],
                                                    w2[:, c, f], start=(f == 0), stop=(f == FC - 1), skip_group_check=True)
                    last.then_inc(s.dn, 1)

            @block.scalar
            def _(act):
                act.wait_ge(s.v, 3)
                nc.scalar.activation(gt[:], lg[:], ACT.Exp).then_inc(s.ex, 1)
                act.wait_ge(s.w1, 32)
                n = 0
                for a in range(5):
                    for f in range(FC):
                        act.wait_ge(s.up, n + 1)
                        nc.scalar.activation(hc[a][:, f], up_ps[n % 4][:, 0:len(USERS[a]) * IMAGES], ACT.Gelu,
                                             bias=b1[:, a, f:f + 1]).then_inc(s.hc, 1)
                        n += 1

            @block.vector
            def _(dve):
                own = Own(dve, s.v)

                def two(r):
                    return r[:].unsqueeze(2).broadcast_to([IMAGES, CLS, 2])
                dve.wait_ge(s.g, 1)
                own.link(nc.vector.tensor_copy(lg[:], pg[0:IMAGES, 0:2 * CLS].rearrange("p (i k) -> p i k", k=2)))
                own.link(nc.vector.tensor_reduce(r1[:], lg[:], AX.X, ALU.max))
                own.link(nc.vector.tensor_tensor(lg[:], lg[:], two(r1), ALU.subtract))
                dve.wait_ge(s.ex, 1)
                own.link(nc.vector.tensor_reduce(r1[:], gt[:], AX.X, ALU.add))
                own.link(nc.vector.reciprocal(r2[:], r1[:]))
                own.link(nc.vector.tensor_tensor(gt[:], gt[:], two(r2), ALU.mult))
                own.link(nc.vector.tensor_reduce(r1[:], gt[:], AX.X, ALU.min))
                own.link(nc.vector.tensor_tensor(mk[:], gt[:], two(r1), ALU.is_gt))
                own.link(nc.vector.tensor_tensor(gt[:], gt[:], mk[:], ALU.mult))
                own.link(nc.vector.tensor_reduce(r1[:], gt[:], AX.X, ALU.add))
                own.link(nc.vector.tensor_scalar(r1[:], r1[:], 1e-6, None, ALU.max))
                own.link(nc.vector.reciprocal(r2[:], r1[:]))
                own.link(nc.vector.tensor_tensor(gt[:], gt[:], two(r2), ALU.mult))
                dve.wait_ge(s.w2, 32)
                for i in range(CLS):
                    dve.wait_ge(s.dn, i + 1)
                    nc.vector.tensor_tensor(tmp[:, i], dn_ps[i % 3][0:IMAGES, 0:2 * D].rearrange("p (k d) -> p k d", k=2),
                                            b2[:, i], ALU.add).then_inc(s.tm, 1)
                    dve.wait_ge(s.tm, i + 1)
                    own.link(nc.vector.tensor_scalar(co[:, i], tmp[:, i, 0], gt[:, i, 0:1], None, ALU.mult))
                    nc.vector.scalar_tensor_tensor(co[:, i], tmp[:, i, 1], gt[:, i, 1:2], co[:, i],
                                                   ALU.mult, ALU.add).then_inc(s.co, 1)
                dve.wait_ge(s.ld, 32)
                nc.vector.tensor_tensor(R.h[:], R.h[:], dl[:], ALU.add)



DI, NS, RANK = 2 * D, 16, 12
DC = DI // P
SB = BLK // SEQ
DIRS = 2


def mamba(nc, R, I):
    with Mem(nc, "m3") as m:
        yg = m.sb("yg", [P, DC, DIRS * TOK])
        with Mem(nc, "m3x") as mx:
            xp = mx.sb("xp", [KP, KC, DIRS * TOK])
            mamba_in(nc, R, I, xp)
            mamba_scan(nc, R, I, xp, yg)
        mamba_out(nc, R, I, yg)


def mamba_in(nc, R, I, xp):
    with Mem(nc, "mi") as m:
        w = m.sb("w", [KP, KC, DIRS * KC * KP])
        b = m.sb("b", [KP, DIRS * KC])
        ps = [m.ps(f"p{k}", [P, 512]) for k in range(8)]
        work = [(d, k, q) for d in range(DIRS) for k in range(KC) for q in range(NB)]
        with phase(nc, "mi", "w", "mm", "a", "v") as (block, s):
            @block.sync
            def _(sp):
                sp.dma_start(w[:], I["m_bi_w"]).then_inc(s.w, 16)
                sp.dma_start(b[:], I["m_bi_b"]).then_inc(s.w, 16)

            @block.tensor
            def _(pe):
                pe.wait_ge(s.w, 32)
                for n, (d, k, q) in enumerate(work):
                    if n >= 8:
                        pe.wait_ge((s.a, s.v)[n % 2], (n - 8) // 2 + 1)
                    for c in range(KC):
                        o = (d * KC + k) * KP
                        last = nc.tensor.matmul(ps[n % 8][0:KP, :], w[:, c, o:o + KP], R.xnT[:, c, q * BLK:(q + 1) * BLK],
                                                start=(c == 0), stop=(c == KC - 1))
                    last.then_inc(s.mm, 1)

            def ends(n):
                d, k, q = work[n]
                dst = xp[:, k, d * TOK + q * BLK:d * TOK + (q + 1) * BLK].rearrange("p (i t) -> p i t", t=SEQ)
                if d == 1:
                    dst = dst[:, :, ::-1]
                src = ps[n % 8][0:KP, :].rearrange("p (i t) -> p i t", t=SEQ)
                return dst, src, b[:, d * KC + k:d * KC + k + 1]

            @block.scalar
            def _(act):
                act.wait_ge(s.w, 32)
                for n in range(0, len(work), 2):
                    act.wait_ge(s.mm, n + 1)
                    dst, src, bias = ends(n)
                    nc.scalar.activation(dst, src, ACT.Identity, bias=bias).then_inc(s.a, 1)

            @block.vector
            def _(dve):
                dve.wait_ge(s.w, 32)
                for n in range(1, len(work), 2):
                    dve.wait_ge(s.mm, n + 1)
                    dst, src, bias = ends(n)
                    nc.vector.tensor_scalar(dst, src, bias, None, ALU.add).then_inc(s.v, 1)


def mamba_scan(nc, R, I, xp, yg):
    with Mem(nc, "ms") as m:
        win = m.sb("win", [KP, KC, 2 * DI])
        cw = m.sb("cw", [P, DC, 4])
        cb = m.sb("cb", [P, DC])
        xw = m.sb("xw", [P, DC, 96])
        dw = m.sb("dw", [RANK, DI])
        db = m.sb("db", [P, DC])
        A = m.sb("A", [P, DC, NS])
        Dp = m.sb("Dp", [P, DC])
        sel = m.sb("sel", [96, NS, P])
        xc = m.sb("xc", [P, DC, SB, SEQ + 3])
        cv = m.sb("cv", [P, DC, BLK])
        zs = m.sb("zs", [P, DC, BLK])
        u = m.sb("u", [P, DC, BLK])
        pj = m.sb("pj", [96, BLK])
        dt = m.sb("dt", [P, DC, BLK])
        du = m.sb("du", [P, DC, BLK])
        xb, ln = cv, du
        RD = 3
        dA = m.sb("dA", [P, RD, BLK])
        dB = m.sb("dB", [P, RD, BLK])
        hs = m.sb("hs", [P, RD, BLK])
        hC = m.sb("hC", [P, RD, BLK])
        Cs = m.sb("Cs", [P, 2, BLK])
        wk = [m.ps(f"w{k}", [P, 512]) for k in range(4)]
        py = [m.ps(f"y{k}", [P, 512]) for k in range(DC)]
        NBLK = DIRS * NB
        ST = NS * DC

        def seqs(ap):
            return ap.rearrange("p (i t) -> p i t", t=SEQ)

        with phase(nc, "ms", "w", "c", "A", "z0", "xz", "ev", "cv", "u", "pp", "pj", "dp", "sp", "dt",
                   "bc", "cs", "bu", "ea", "hh", "hc", "yy", "out", "yd", "v") as (block, s):
            @block.sync
            def _(sp):
                for dst, name in ((win, "m_win"), (cw, "m_cw"), (cb, "m_cb"), (xw, "m_xw"), (dw, "m_dw"),
                                  (db, "m_db"), (A, "m_A"), (Dp, "m_D")):
                    sp.dma_start(dst[:], I[name]).then_inc(s.w, 16)
            WN = 8 * 16

            @block.gpsimd
            def _(pool):
                nc.gpsimd.memset(sel[:], 0.0).then_inc(s.c, 1)
                nc.gpsimd.memset(xc[:], 0.0).then_inc(s.c, 1)
                nc.gpsimd.memset(dA[:], 0.0).then_inc(s.c, 1)
                for n, k in ((3, 32), (4, 64)):
                    pool.wait_ge(s.c, n)
                    nc.gpsimd.affine_select(out=sel[k:k + NS], in_=sel[k:k + NS], compare_op=ALU.not_equal, fill=1.0,
                                            base=0, pattern=[[-1, NS], [0, P]], channel_multiplier=1).then_inc(s.c, 1)
                pool.wait_ge(s.c, 5)
                with pool.Fori(0, NBLK) as i:
                    for n in range(NS):
                        for c in range(DC):
                            q = n * DC + c
                            pool.wait_ge(s.hh, i * ST + (q + 1) + 1)
                            if c == 0:
                                pool.wait_ge(s.cs, i * NS + (n + 1) + 1)
                            pool.wait_ge(s.yy, i * ST + (q + 1))
                            nc.gpsimd.tensor_tensor(hC[:, q % RD], hs[:, q % RD], Cs[:, n % 2], ALU.mult).then_inc(s.hc, 1)

            @block.tensor
            def _(pe):
                pe.wait_ge(s.w, WN)
                pe.wait_ge(s.c, 5)
                nc.tensor.sem_inc(s.yy, RD)
                nc.tensor.sem_inc(s.bc, 1)
                with pe.Fori(0, NBLK) as i:
                    for g in range(6):
                        pe.wait_ge(s.ev, i * 6 + (g + 1))
                        if g == 0:
                            pe.wait_ge(s.cs, i * NS + 1)
                            pe.wait_ge(s.bu, i * ST + 1)
                        for c in range(KC):
                            last = nc.tensor.matmul(wk[g % 4][:], win[:, c, g * P:(g + 1) * P],
                                                    xp[:, c, bass.ds(i * BLK, BLK)], start=(c == 0), stop=(c == KC - 1))
                        last.then_inc(s.xz, 1)
                    pe.wait_ge(s.u, i * DC + DC)
                    for c in range(DC):
                        last = nc.tensor.matmul(wk[2][0:96, :], xw[:, c], u[:, c], start=(c == 0), stop=(c == DC - 1))
                    last.then_inc(s.pp, 1)
                    pe.wait_ge(s.pj, i + 1)
                    pe.wait_ge(s.ev, i * 6 + 10)
                    for c in range(DC):
                        nc.tensor.matmul(wk[(0, 1, 3)[c]][:], dw[:, c * P:(c + 1) * P], pj[0:RANK, :],
                                         start=True, stop=True).then_inc(s.dp, 1)
                    pe.wait_ge(s.sp, i * DC + DC)

                    def rows(n):
                        if n >= 2:
                            pe.wait_ge(s.bu, i * ST + (n - 1) * DC + 1)
                            pe.wait_ge(s.cs, i * NS + (n - 1) + 1)
                        for k in range(2):
                            r = slice(32 + 32 * k, 32 + 32 * k + NS)
                            last = nc.tensor.matmul(wk[2 * (n % 2) + k][:], sel[r, n], pj[r, :], start=True, stop=True)
                        last.then_inc(s.bc, 1)
                    rows(0)
                    rows(1)
                    pe.wait_ge(s.out, i * DC + 1)
                    for n in range(NS):
                        for c in range(DC):
                            pe.wait_ge(s.hc, i * ST + (n * DC + c + 1))
                            nc.tensor.matmul(py[c][:], R.ident[:], hC[:, (n * DC + c) % RD],
                                             start=(n == 0), stop=(n == NS - 1)).then_inc(s.yy, 1)
                        if n + 2 < NS:
                            rows(n + 2)

            @block.scalar
            def _(act):
                act.wait_ge(s.w, WN)
                nc.scalar.activation(A[:], A[:], ACT.Exp).then_inc(s.A, 1)
                act.wait_ge(s.A, 1)
                nc.scalar.mul(A[:], A[:], -1.0).then_inc(s.A, 1)
                act.wait_ge(s.A, 2)
                act.wait_ge(s.c, 3)
                nc.scalar.sem_inc(s.ev, 4)
                for sem in (s.cs, s.ea):
                    nc.scalar.sem_inc(sem, 1)
                with act.Fori(0, NBLK) as i:
                    for g in range(6):
                        act.wait_ge(s.xz, i * 6 + (g + 1))
                        if g < DC:
                            act.wait_ge(s.cv, i * DC + 1)
                            nc.scalar.activation(xc[:, g, :, 3:], seqs(wk[g % 4][:]), ACT.Copy).then_inc(s.ev, 1)
                        else:
                            act.wait_ge(s.yd, i * DC + 1)
                            nc.scalar.activation(zs[:, g - DC], wk[g % 4][:], ACT.Silu).then_inc(s.ev, 1)
                    for c in range(DC):
                        act.wait_ge(s.cv, i * DC + (c + 1) + 1)
                        nc.scalar.activation(u[:, c], cv[:, c], ACT.Silu).then_inc(s.u, 1)
                    act.wait_ge(s.pp, i + 1)
                    act.wait_ge(s.bc, i * NS + 1)
                    nc.scalar.activation(pj[:], wk[2][0:96, :], ACT.Copy).then_inc(s.pj, 1)
                    for c in range(DC):
                        act.wait_ge(s.dp, i * DC + (c + 1))
                        nc.scalar.activation(xb[:, c], wk[(0, 1, 3)[c]][:], ACT.Identity, bias=db[:, c:c + 1]).then_inc(s.sp, 1)
                    act.wait_ge(s.sp, i * DC + DC)
                    nc.scalar.activation(ln[:], xb[:], ACT.Abs).then_inc(s.A, 1)
                    act.wait_ge(s.A, i * 2 + 3)
                    nc.scalar.activation(ln[:], ln[:], ACT.Exp, scale=-1.0).then_inc(s.A, 1)
                    act.wait_ge(s.A, i * 2 + 4)
                    nc.scalar.activation(ln[:], ln[:], ACT.Ln, bias=1.0).then_inc(s.z0, 1)
                    act.wait_ge(s.dt, i * 2 + 1)
                    for n in range(NS):
                        act.wait_ge(s.bc, i * NS + (n + 1) + 1)
                        if n >= 2:
                            act.wait_ge(s.hc, i * ST + (n - 1) * DC)
                        nc.scalar.activation(Cs[:, n % 2], wk[2 * (n % 2) + 1][:], ACT.Copy).then_inc(s.cs, 1)
                        for c in range(DC):
                            q = n * DC + c
                            if q >= RD:
                                act.wait_ge(s.hh, i * ST + (q - RD + 1) + 1)
                            nc.scalar.activation(seqs(dA[:, q % RD])[:, :, 1:], seqs(dt[:, c])[:, :, 1:], ACT.Exp,
                                                 scale=A[:, c, n:n + 1]).then_inc(s.ea, 1)

            @block.vector
            def _(dve):
                dve.wait_ge(s.w, WN)
                for sem in (s.hh, s.bu, s.out, s.cv, s.yd):
                    nc.vector.sem_inc(sem, 1)
                with dve.Fori(0, NBLK) as i:
                    PER = 3 * DC
                    for c in range(DC):
                        dve.wait_ge(s.ev, i * 6 + (c + 5))
                        dve.wait_ge(s.yd, i * DC + 1)
                        for k in range(4):
                            if k == 0:
                                ins = nc.vector.tensor_scalar(seqs(cv[:, c]), xc[:, c, :, 0:SEQ], cw[:, c, 0:1],
                                                              cb[:, c:c + 1], ALU.mult, ALU.add)
                            else:
                                ins = nc.vector.scalar_tensor_tensor(seqs(cv[:, c]), xc[:, c, :, k:k + SEQ], cw[:, c, k:k + 1],
                                                                     seqs(cv[:, c]), ALU.mult, ALU.add)
                            if k < 3:
                                ins.then_inc(s.v, 1)
                                dve.wait_ge(s.v, i * PER + (c * 3 + k + 1))
                            else:
                                ins.then_inc(s.cv, 1)
                    dve.wait_ge(s.z0, i + 1)
                    dve.wait_ge(s.ea, i * ST + 1)
                    nc.vector.scalar_tensor_tensor(dt[:], xb[:], 0.0, ln[:], ALU.max, ALU.add).then_inc(s.dt, 1)
                    dve.wait_ge(s.dt, i * 2 + 1)
                    nc.vector.tensor_tensor(du[:], dt[:], u[:], ALU.mult).then_inc(s.dt, 1)
                    dve.wait_ge(s.dt, i * 2 + 2)
                    for n in range(NS):
                        dve.wait_ge(s.bc, i * NS + (n + 1) + 1)
                        for c in range(DC):
                            q = n * DC + c
                            dve.wait_ge(s.hh, i * ST + max(q - RD + 1, 0) + 1)
                            nc.vector.tensor_tensor(dB[:, q % RD], wk[2 * (n % 2)][:], du[:, c], ALU.mult).then_inc(s.bu, 1)
                        for c in range(DC):
                            q = n * DC + c
                            dve.wait_ge(s.bu, i * ST + (q + 1) + 1)
                            dve.wait_ge(s.ea, i * ST + (q + 1) + 1)
                            if q >= RD:
                                dve.wait_ge(s.hc, i * ST + (q - RD + 1))
                            nc.vector.tensor_tensor_scan(hs[:, q % RD], dA[:, q % RD], dB[:, q % RD], 0.0,
                                                         ALU.mult, ALU.add).then_inc(s.hh, 1)
                    dve.wait_ge(s.yy, i * ST + (ST + RD))
                    for c in range(DC):
                        nc.vector.scalar_tensor_tensor(cv[:, c], u[:, c], Dp[:, c:c + 1], py[c][:],
                                                       ALU.mult, ALU.add).then_inc(s.out, 1)
                    dve.wait_ge(s.out, i * DC + DC + 1)
                    for c in range(DC):
                        nc.vector.tensor_tensor(yg[:, c, bass.ds(i * BLK, BLK)], cv[:, c], zs[:, c], ALU.mult).then_inc(s.yd, 1)


def mamba_out(nc, R, I, yg):
    with Mem(nc, "mo") as m:
        wo = m.sb("wo", [P, DC, D])
        wb = m.sb("wb", [KP, KC, D])
        rowsb = m.sb("rows", [P, 3, D])
        oT = m.sb("oT", [KP, KC, TOK])
        y = m.sb("y", [P, TILES, D])
        st = m.sb("st", [P, TILES, nc.vector.BN_STATS_DIM])
        mv = m.sb("mv", [P, TILES, nc.vector.BN_AGGR_DIM])
        sd = m.sb("sd", [P, TILES])
        rs = m.sb("rs", [P, TILES])
        ps = [m.ps(f"p{k}", [P, 512]) for k in range(8)]
        with phase(nc, "mo", "w", "y", "mm", "ot", "xb", "m2", "v", "sd", "st") as (block, s):
            @block.sync
            def _(sp):
                sp.dma_start(wo[:], I["m_wo"]).then_inc(s.w, 16)
                sp.dma_start(wb[:], I["m_bo_w"]).then_inc(s.w, 16)
                sp.dma_start(rowsb[:], I["m_rows"].unsqueeze(0).broadcast_to([P, 3, D])).then_inc(s.w, 16)

            def fwd(c):
                return yg[:, c, 0:TOK].rearrange("p (i t) -> p i t", t=SEQ)

            def bwd(c):
                return yg[:, c, TOK:2 * TOK].rearrange("p (i t) -> p i t", t=SEQ)[:, :, ::-1]

            @block.gpsimd
            def _(pool):
                pool.wait_ge(s.w, 48)
                nc.gpsimd.tensor_tensor(R.xn[:], R.xn[:], rowsb[:, 0].unsqueeze(1).broadcast_to([P, TILES, D]),
                                        ALU.add).then_inc(s.xb, 1)

            @block.tensor
            def _(pe):
                pe.wait_ge(s.w, 48)
                pe.wait_ge(s.y, DC)
                for n in range(NB * KC):
                    b, k = divmod(n, KC)
                    for c in range(DC):
                        last = nc.tensor.matmul(ps[n][0:KP, :], wo[:, c, k * KP:(k + 1) * KP], yg[:, c, b * BLK:(b + 1) * BLK],
                                                start=(c == 0), stop=(c == DC - 1))
                    last.then_inc(s.mm, 1)
                for t in range(TILES):
                    if t % 4 == 0:
                        pe.wait_ge(s.ot, min(2 * (t // 4) + 2, 8))
                    pe.wait_ge(s.ot, t + 1 if t < 8 else 8)
                    if t >= 8:
                        pe.wait_ge(s.v, t - 7)
                    for c in range(KC):
                        last = nc.tensor.matmul(ps[t % 8][:, 0:D], oT[:, c, t * P:(t + 1) * P], wb[:, c],
                                                start=(c == 0), stop=(c == KC - 1))
                    last.then_inc(s.m2, 1)

            @block.scalar
            def _(act):
                for n in range(NB * KC):
                    b, k = divmod(n, KC)
                    act.wait_ge(s.mm, n + 1)
                    nc.scalar.activation(oT[:, k, b * BLK:(b + 1) * BLK], ps[n][0:KP, :], ACT.Copy).then_inc(s.ot, 1)
                act.wait_ge(s.st, 2)
                nc.scalar.activation(sd[:], mv[:, :, 1], ACT.Sqrt, bias=R.eps[:]).then_inc(s.sd, 1)

            @block.vector
            def _(dve):
                for c in range(DC):
                    nc.vector.tensor_tensor(fwd(c), fwd(c), bwd(c), ALU.add).then_inc(s.y, 1)
                dve.wait_ge(s.xb, 1)
                for t in range(TILES):
                    dve.wait_ge(s.m2, t + 1)
                    nc.vector.tensor_tensor(y[:, t], ps[t % 8][:, 0:D], R.xn[:, t], ALU.add).then_inc(s.v, 1)
                dve.wait_ge(s.v, TILES)
                for t in range(TILES):
                    last = nc.vector.bn_stats(st[:, t], y[:, t])
                last.then_inc(s.st, 1)
                dve.wait_ge(s.st, 1)
                for t in range(TILES):
                    last = nc.vector.bn_aggr(mv[:, t], st[:, t])
                last.then_inc(s.st, 1)
                dve.wait_ge(s.sd, 1)
                nc.vector.reciprocal(rs[:], sd[:]).then_inc(s.v, 1)
                dve.wait_ge(s.v, TILES + 1)
                for t in range(TILES):
                    nc.vector.tensor_scalar(y[:, t], y[:, t], mv[:, t, 0:1], rs[:, t:t + 1], ALU.subtract, ALU.mult)
                def all_tiles(k):
                    return rowsb[:, k].unsqueeze(1).broadcast_to([P, TILES, D])
                own = Own(dve, s.v)
                own.n = TILES + 1
                own.link(nc.vector.tensor_tensor(R.h[:], R.h[:], all_tiles(2), ALU.add))
                own.link(nc.vector.tensor_tensor(y[:], y[:], all_tiles(1), ALU.mult))
                nc.vector.tensor_tensor(R.h[:], R.h[:], y[:], ALU.add)



def ffn3(nc, R, I):
    E = 8
    with Mem(nc, "f3") as m:
        coef = m.sb("coef", [P, TILES, E])
        acc = m.sb("acc", [P, TILES, D])
        top = m.sb("top", [P, TILES, 8])
        with Mem(nc, "f3r") as r:
            wr = r.sb("wr", [KP, KC, E])
            rb = r.sb("rb", [P, E])
            io = r.sb("io", [P, E])
            lg = r.sb("lgs", [P, TILES, E])
            mx = r.sb("mx", [P, TILES])
            sm = r.sb("sm", [P, TILES])
            idx = r.sb("idx", [P, TILES, 8], U32)
            idf = r.sb("idf", [P, TILES, 8])
            ps = r.ps("lg", [P, 512])
            with phase(nc, "f3r", "w", "io", "lg", "v", "ex") as (block, s):
                @block.sync
                def _(sp):
                    sp.dma_start(wr[:], I["f3_wr"]).then_inc(s.w, 16)
                    sp.dma_start(rb[:], row(I["f3_rb"])).then_inc(s.w, 16)

                @block.gpsimd
                def _(pool):
                    nc.gpsimd.iota(io[:], [[1, E]], base=0, channel_multiplier=0,
                                   allow_small_or_imprecise_dtypes=True).then_inc(s.io, 1)
                    nc.gpsimd.memset(acc[:], 0.0)

                @block.tensor
                def _(pe):
                    pe.wait_ge(s.w, 32)
                    logits(nc, pe, R, ps, wr, E).then_inc(s.lg, 1)

                @block.scalar
                def _(act):
                    act.wait_ge(s.v, 3)
                    nc.scalar.activation(lg[:], lg[:], ACT.Exp).then_inc(s.ex, 1)

                @block.vector
                def _(dve):
                    own = Own(dve, s.v)

                    def over(a):
                        return a.unsqueeze(2).broadcast_to([P, TILES, E])
                    dve.wait_ge(s.w, 32)
                    dve.wait_ge(s.lg, 1)
                    own.link(nc.vector.tensor_tensor(lg[:], ps[:, 0:TILES * E].rearrange("p (t e) -> p t e", e=E),
                                                     rb[:].unsqueeze(1).broadcast_to([P, TILES, E]), ALU.add))
                    own.link(nc.vector.tensor_reduce(mx[:], lg[:], AX.X, ALU.max))
                    own.link(nc.vector.tensor_tensor(lg[:], lg[:], over(mx[:]), ALU.subtract))
                    dve.wait_ge(s.ex, 1)
                    own.link(nc.vector.tensor_reduce(mx[:], lg[:], AX.X, ALU.add))
                    own.link(nc.vector.reciprocal(sm[:], mx[:]))
                    own.link(nc.vector.tensor_tensor(lg[:], lg[:], over(sm[:]), ALU.mult))
                    for t in range(TILES):
                        own.mark(nc.vector.max(top[:, t], lg[:, t]))
                    own.settle()
                    for t in range(TILES):
                        last = nc.vector.max_index(idx[:, t], top[:, t], lg[:, t])
                    own.link(last)
                    own.link(nc.vector.tensor_copy(idf[:], idx[:]))
                    dve.wait_ge(s.io, 1)
                    nc.vector.tensor_tensor(coef[:], io[:].unsqueeze(1).broadcast_to([P, TILES, E]),
                                            idf[:, :, 0:1].broadcast_to([P, TILES, E]), ALU.is_equal)
        experts(nc, R, "f3e", E, 512, I["f3_up"], I["f3_down"], ACT.Silu, True,
                lambda t, e: coef[:, t, bass.ds(e, 1)], acc[:])
        half = m.sb("half", [P, TILES, D], BF16)
        with phase(nc, "f3f", "v") as (block, s):
            @block.vector
            def _(dve):
                nc.vector.tensor_copy(half[:], acc[:]).then_inc(s.v, 1)
                dve.wait_ge(s.v, 1)
                for t in range(TILES):
                    nc.vector.scalar_tensor_tensor(R.h[:, t], half[:, t], top[:, t, 0:1], R.h[:, t], ALU.mult, ALU.add)


def expert_up(w):
    return w.transpose(0, 2, 1).reshape(len(w), KC, KP, -1).transpose(0, 2, 1, 3)


def expert_down(w):
    return w.reshape(len(w), -1, P, D).transpose(0, 2, 1, 3)


def more_layout(a, z):
    z["f0_wr"] = chunked(a["L0_ffn_Wr"].T)
    z["f0_bo"] = a["L0_ffn_bo"]
    z["f0_up"] = expert_up(a["L0_ffn_Wi"])
    z["f0_down"] = expert_down(a["L0_ffn_Wo"].transpose(0, 2, 1))
    z["f0_bi"] = a["L0_ffn_bi"].reshape(8, -1, P).transpose(0, 2, 1)
    def rotary(w):
        return w.reshape(HEADS, -1, 32, 2).transpose(1, 3, 0, 2).reshape(w.shape[1], -1)
    z["a1_wT"] = chunked(np.concatenate([rotary(a["L1_attn_W_Q"]), rotary(a["L1_attn_W_K"])], 1))
    z["a1_bT"] = grouped(np.concatenate([rotary(a["L1_attn_b_Q"][:, None])[0], rotary(a["L1_attn_b_K"][:, None])[0]]))
    z["a1_wV"] = chunked(a["L1_attn_W_V"].transpose(1, 0, 2).reshape(D, -1))
    z["a1_bV"] = a["L1_attn_b_V"].reshape(-1)
    z["a1_wO"] = a["L1_attn_W_O"].reshape(6, P, D).transpose(1, 0, 2)
    z["a1_bO"] = a["L1_attn_b_O"]
    z["a1_tri"] = np.tile(np.tril(np.ones((SEQ, SEQ), np.float32)), (2, 1))
    freq = (np.float32(1.0) / np.float32(10000.0) ** (np.arange(0, 64, 2, dtype=np.float32) / np.float32(64))).astype(np.float32)
    ang = np.arange(SEQ, dtype=np.float32)[None, :] * freq[:, None]
    z["a1_cs"] = np.tile(np.stack([np.cos(ang), np.sin(ang)], 1), (4, 1, 1)).astype(np.float32)
    z["f1_gate"] = chunked(a["L1_ffn_gate_weight"].T)
    z["f1_up"] = np.concatenate([expert_up(a["L1_ffn_Wg"]), expert_up(a["L1_ffn_Wu"])], 3)
    z["f1_down"] = expert_down(a["L1_ffn_Wd"].transpose(0, 2, 1))
    z["f1_sup"] = np.concatenate([expert_up(a["L1_ffn_Ws_g"][None]), expert_up(a["L1_ffn_Ws_u"][None])], 3)
    z["f1_sdown"] = expert_down(a["L1_ffn_Ws_d"].T[None])
    hd = D // HEADS
    wq, wk, wv = np.split(a["L2_attn_w_qkv"].T, 3, axis=1)
    z["a2_wT"] = chunked(np.concatenate([head_pad(wq, hd), head_pad(wk, hd)], 1))
    z["a2_wV"] = chunked(head_pad(wv, hd))
    z["a2_wO"] = head_pad(a["L2_attn_w_proj"], hd).T.reshape(3, P, D).transpose(1, 0, 2)
    z["a2_bO"] = a["L2_attn_b_proj"]
    z["f2_patch"] = ((np.arange(P) % SEQ) >= CLS).astype(np.float32)[:, None]
    z["f2_up"] = chunked(a["L2_ffn_moe0_W1"])[None]
    z["f2_down"] = expert_down(a["L2_ffn_moe0_W2"][None])
    z["f2_bi"] = grouped(a["L2_ffn_moe0_b1"])[None]
    z["f2_b2"] = a["L2_ffn_moe0_b2"]
    z["f2_a1"] = a["L2_ffn_A1_W"].reshape(5, KC, KP, -1).transpose(2, 0, 1, 3)
    z["f2_a1b"] = a["L2_ffn_A1_b"].reshape(5, -1, P).transpose(2, 0, 1)
    z["f2_a2"] = a["L2_ffn_A2_W"].reshape(5, -1, P, D).transpose(2, 0, 1, 3)
    z["f2_a2b"] = np.stack([a["L2_ffn_A2_b"][[c1, c0]] for c0, c1 in CLS_PAIRS])
    z["f2_gw"] = a["L2_ffn_G_W"].reshape(CLS, KC, KP, 2).transpose(2, 1, 0, 3)
    z["m_bi_w"] = chunked(a["L3_attn_bm_in_w"].T)
    z["m_bi_b"] = a["L3_attn_bm_in_b"].reshape(-1, KP).T
    z["m_win"] = chunked(a["L3_attn_m_in_w"].T)
    z["m_cw"] = a["L3_attn_m_conv_w"].reshape(DC, P, 4).transpose(1, 0, 2)
    z["m_cb"] = grouped(a["L3_attn_m_conv_b"])
    xw = a["L3_attn_m_xproj_w"].T
    pad = np.zeros((DI, 96), xw.dtype)
    pad[:, 0:RANK], pad[:, 32:32 + NS], pad[:, 64:64 + NS] = xw[:, :RANK], xw[:, RANK:RANK + NS], xw[:, RANK + NS:]
    z["m_xw"] = pad.reshape(DC, P, 96).transpose(1, 0, 2)
    z["m_dw"] = a["L3_attn_m_dt_w"].T
    z["m_db"] = grouped(a["L3_attn_m_dt_b"])
    z["m_A"] = a["L3_attn_m_A_log"].reshape(DC, P, NS).transpose(1, 0, 2)
    z["m_D"] = grouped(a["L3_attn_m_D"])
    z["m_wo"] = a["L3_attn_m_out_w"].T.reshape(DC, P, D).transpose(1, 0, 2)
    z["m_bo_w"] = chunked(a["L3_attn_bm_out_w"].T)
    z["m_rows"] = np.stack([a["L3_attn_bm_out_b"], a["L3_attn_ln_g"], a["L3_attn_ln_b"]])
    z["f3_wr"] = chunked(a["L3_ffn_router_w"])
    z["f3_rb"] = a["L3_ffn_router_b"]
    def up(w):
        return w.reshape(len(w), KC, KP, -1).transpose(0, 2, 1, 3)
    z["f3_up"] = np.concatenate([up(a["L3_ffn_w1"]), up(a["L3_ffn_w2"])], 3)
    z["f3_down"] = expert_down(a["L3_ffn_w3"])



def attention0(nc, R, I):
    with Mem(nc, "a0") as m:
        qk = m.sb("qk", [P, 6, TOK])
        V = m.sb("V", [P, TILES, 12 * 32])
        aT = m.sb("aT", [P, 3, TOK])
        project_heads(nc, R, "a0p", I["a0_wT"], I["a0_bT"], [qk[:, g] for g in range(6)], I["a0_wV"], I["a0_bV"], V[:])
        attend(nc, R, "a0a", [(qk[:, 0:3], qk[:, 3:6])], D // HEADS, (D // HEADS) ** -0.5, V[:], 32, aT[:])
        project_out(nc, R, "a0o", aT, 3, I["a0_wO"], I["a0_bO"])


def program(nc, I, out, stages=None, h_in=None):
    with ExitStack() as st:
        R = Resident()
        R.ident = st.enter_context(nc.sbuf_tensor("ident", [P, P], F32))
        R.ones = st.enter_context(nc.sbuf_tensor("ones", [P, P], F32))
        R.eps = st.enter_context(nc.sbuf_tensor("eps", [P, 1], F32))
        R.h = st.enter_context(nc.sbuf_tensor("h", [P, TILES, D], F32))
        R.xn = st.enter_context(nc.sbuf_tensor("xn", [P, TILES, D], F32))
        R.xnT = st.enter_context(nc.sbuf_tensor("xnT", [KP, KC, TOK], F32))
        constants(nc, R)
        if h_in is not None:
            with phase(nc, "hin", "d") as (block, s):
                @block.sync
                def _(sp):
                    sp.dma_start(R.h[:], h_in.rearrange("(t p) d -> p t d", p=P)).then_inc(s.d, 16)
                    sp.wait_ge(s.d, 16)
        def on(name):
            return stages is None or name in stages
        if on("tok"):
            tokenizer(nc, R, I["x"], I["tok_w"], I["tok_ln"], I["tok_mult"], I["tok_b"])
        if on("a0"):
            normalise(nc, R, "n0")
            attention0(nc, R, I)
        for name, layer in (("f0", ffn0), ("a1", attention1), ("f1", ffn1), ("a2", attention2), ("f2", ffn2),
                            ("a3", mamba), ("f3", ffn3)):
            if on(name):
                normalise(nc, R, "n" + name)
                layer(nc, R, I)
        with phase(nc, "out", "d") as (block, s):
            @block.sync
            def _(sp):
                sp.dma_start(out.rearrange("(t p) d -> p t d", p=P), R.h[:]).then_inc(s.d, 16)
                sp.wait_ge(s.d, 16)



def kernel(**inputs):
    import concourse.bacc as bacc
    from concourse.bass_utils import run_bass_kernel_spmd

    arrays = layout({k: np.asarray(v) for k, v in inputs.items()})
    nc = bacc.Bacc("TRN2", target_bir_lowering=False, num_devices=1)
    I = {k: nc.dram_tensor(f"in_{k}", v.shape, mybir.dt.from_np(v.dtype), kind="ExternalInput").ap()
         for k, v in arrays.items()}
    out = nc.dram_tensor("tokens_out", (TOK, D), F32, kind="ExternalOutput").ap()
    program(nc, I, out)
    got = run_bass_kernel_spmd(nc, [{f"in_{k}": v for k, v in arrays.items()}], core_ids=[0])
    return got.results[0]["tokens_out"].reshape(IMAGES, SEQ, D)
```
